# Optimizing a Trainium2 kernel written in Bass

```python
import numpy as np
import jax
import jax.numpy as jnp

def _softmax(x, axis=-1):
    return jax.nn.softmax(x, axis=axis)

def _gelu(x):
    return jax.nn.gelu(x, approximate=True)

def _silu(x):
    return jax.nn.silu(x)

def _sigmoid(x):
    return jax.nn.sigmoid(x)

def _layernorm(x, axis=-1, eps=1e-05):
    m = jnp.mean(x, axis=axis, keepdims=True)
    v = jnp.var(x, axis=axis, keepdims=True)
    return (x - m) / jnp.sqrt(v + eps)

def _scatter_add(tgt, idx, src, axis=0):
    return tgt.at[idx].add(src)

def _segment_sum(src, seg, n):
    return jax.ops.segment_sum(src, seg, n)
kernel_name = 'mk_adj_resnorm_d4_adj_r2_56110e'

def setup_inputs(seed: int=0):
    np.random.seed(seed)
    _w = jnp.asarray

    def _rec_inputs():
        import jax
        import jax.numpy as jnp
        _gk = jax.random.key(seed)
        x = 7.22e-05 + 1 * jax.random.normal(jax.random.fold_in(_gk, 1), (8, 2048, 64), jnp.float32)
        _a = jax.random.bernoulli(jax.random.fold_in(_gk, 2), 0.00390625, (2048, 2048))
        _a = jnp.logical_or(_a, jnp.swapaxes(_a, -1, -2))
        _a = jnp.logical_or(_a, jnp.eye(2048, dtype=bool))
        adj = _a.astype(jnp.int32)
        return (x, adj)
    x, adj = _rec_inputs()

    def _L0_gnn_setup():
        import jax, jax.numpy as jnp
        import numpy as np
        B, N, F_IN, F_OUT = (32, 2048, 64, 64)
        ALPHA = 0.2

        def _xavier(key, shape, gain=1.414):
            fan_in, fan_out = (shape[0], shape[1])
            bound = gain * np.sqrt(6.0 / (fan_in + fan_out))
            return jax.random.uniform(key, shape, jnp.float32, -bound, bound)
        key = jax.random.key(seed)
        k1, k2, k3, k4 = jax.random.split(key, 4)
        inp = jax.random.normal(k1, (B, N, F_IN), jnp.float32)
        W = _xavier(k2, (F_IN, F_OUT))
        a = _xavier(k3, (2 * F_OUT, N))
        adj = jax.random.randint(k4, (N, N), 0, 2, jnp.int32)
        return {'inp': inp, 'W': W, 'a': a, 'adj': adj}
    _L0_gnn_all = _L0_gnn_setup()
    _L0_gnn_in = {k: v for k, v in _L0_gnn_all.items() if k in ('W', 'a')}
    del _L0_gnn_all

    def _L1_gnn_setup():
        import jax, jax.numpy as jnp
        import numpy as np
        NEG = -1e+16
        LN_EPS = 1e-05

        def _gat_layer(h, mask, b):
            scores = jnp.einsum('...nd,...md->...nm', h, h)
            scores = jnp.where(mask, scores, NEG)
            attn = jax.nn.softmax(scores, axis=-1)
            return jnp.einsum('...nm,...md->...nd', attn, h) + b
        key = jax.random.key(seed)
        ks = jax.random.split(key, 6)
        B, N, C, H, D = (8, 1024, 64, 4, 64)
        x = jax.random.normal(ks[0], (B, N, C), dtype=jnp.float32)
        graph = jax.random.randint(ks[1], (N, N), 0, 2, dtype=jnp.int32)
        bnd_h = float(np.sqrt(6.0 / (C + D)))
        Wh = jax.random.uniform(ks[2], (H, D, C), jnp.float32, -bnd_h, bnd_h)
        bh = jnp.zeros((H, D), jnp.float32)
        bnd_o = float(np.sqrt(6.0 / (H * D + D)))
        Wo = jax.random.uniform(ks[3], (D, H * D), jnp.float32, -bnd_o, bnd_o)
        bo = jnp.zeros((D,), jnp.float32)
        gamma = jnp.ones((D,), jnp.float32)
        beta = jnp.zeros((D,), jnp.float32)
        return {'x': x, 'graph': graph, 'Wh': Wh, 'bh': bh, 'Wo': Wo, 'bo': bo, 'gamma': gamma, 'beta': beta}
    _L1_gnn_all = _L1_gnn_setup()
    _L1_gnn_in = {k: v for k, v in _L1_gnn_all.items() if k in ('Wh', 'bh', 'Wo', 'bo', 'gamma', 'beta')}
    del _L1_gnn_all

    def _L2_gnn_setup():
        import jax, jax.numpy as jnp
        import numpy as np
        NEG_INF = -9000000000000000.0
        LEAKY_SLOPE = 0.01
        key = jax.random.key(seed)
        k1, k2, k3, k4 = jax.random.split(key, 4)
        B, N, Fin, Fout = (4, 2048, 64, 64)
        X = jax.random.normal(k1, (B, N, Fin), dtype=jnp.float32)
        A = jax.random.randint(k2, (N, N), 0, 2, dtype=jnp.int32)
        weight = jax.random.normal(k3, (Fin, Fout), dtype=jnp.float32) * 0.15
        a = jax.random.normal(k4, (2 * Fout, 1), dtype=jnp.float32) * 0.15
        return {'X': X, 'A': A, 'weight': weight, 'a': a}
    _L2_gnn_all = _L2_gnn_setup()
    _L2_gnn_in = {k: v for k, v in _L2_gnn_all.items() if k in ('weight', 'a')}
    del _L2_gnn_all

    def _L3_gnn_setup():
        import jax, jax.numpy as jnp
        import numpy as np
        ALPHA = 0.2
        NEG_INF = -1e+30
        key = jax.random.key(seed)
        k1, k2, k3, k4 = jax.random.split(key, 4)
        B, N, Din, Dout = (8, 1024, 64, 64)
        x = jax.random.normal(k1, (B, N, Din), dtype=jnp.float32)
        adj = jax.random.randint(k2, (N, N), 0, 2, dtype=jnp.int32)
        W = jax.random.normal(k3, (Din, Dout), dtype=jnp.float32) * (1.0 / np.sqrt(Din))
        a = jax.random.normal(k4, (2 * Dout,), dtype=jnp.float32) * 0.1
        return {'x': x, 'adj': adj, 'W': W, 'a': a}
    _L3_gnn_all = _L3_gnn_setup()
    _L3_gnn_in = {k: v for k, v in _L3_gnn_all.items() if k in ('W', 'a')}
    del _L3_gnn_all
    return {'x': x, 'adj': adj, 'L0_gnn_W': _L0_gnn_in['W'], 'L0_gnn_a': _L0_gnn_in['a'], 'L1_gnn_Wh': _L1_gnn_in['Wh'], 'L1_gnn_bh': _L1_gnn_in['bh'], 'L1_gnn_Wo': _L1_gnn_in['Wo'], 'L1_gnn_bo': _L1_gnn_in['bo'], 'L1_gnn_gamma': _L1_gnn_in['gamma'], 'L1_gnn_beta': _L1_gnn_in['beta'], 'L2_gnn_weight': _L2_gnn_in['weight'], 'L2_gnn_a': _L2_gnn_in['a'], 'L3_gnn_W': _L3_gnn_in['W'], 'L3_gnn_a': _L3_gnn_in['a']}

def reference(x, adj, L0_gnn_W, L0_gnn_a, L1_gnn_Wh, L1_gnn_bh, L1_gnn_Wo, L1_gnn_bo, L1_gnn_gamma, L1_gnn_beta, L2_gnn_weight, L2_gnn_a, L3_gnn_W, L3_gnn_a):
    import jax
    import jax.numpy as jnp

    def _L0_gnn_ref(inp, W, a, adj):
        import jax, jax.numpy as jnp
        import numpy as np
        B, N, F_IN, F_OUT = (32, 2048, 64, 64)
        ALPHA = 0.2

        def _xavier(key, shape, gain=1.414):
            fan_in, fan_out = (shape[0], shape[1])
            bound = gain * np.sqrt(6.0 / (fan_in + fan_out))
            return jax.random.uniform(key, shape, jnp.float32, -bound, bound)
        h = jnp.matmul(inp, W)
        h = h.at[:, 0, :].set(0.0)
        Do = W.shape[0] if False else W.shape[1]
        mask = (adj[1:, :] > 0).astype(h.dtype)
        h2 = jnp.einsum('ji,bjd->bid', mask, h[:, :-1, :])
        a1, a2 = (a[:Do, :], a[Do:, :])
        score = jnp.einsum('bid,di->bi', h, a1) + jnp.einsum('bid,di->bi', h2, a2)
        score = score.at[:, 0].set(0.0)
        hsum = jnp.sum(h, axis=1, keepdims=True)
        h_prime = score[:, :, None] * hsum
        return jnp.where(h_prime >= 0, h_prime, ALPHA * h_prime)

    def _L1_gnn_ref(x, graph, Wh, bh, Wo, bo, gamma, beta):
        import jax, jax.numpy as jnp
        import numpy as np
        NEG = -1e+16
        LN_EPS = 1e-05

        def _gat_layer(h, mask, b):
            scores = jnp.einsum('...nd,...md->...nm', h, h)
            scores = jnp.where(mask, scores, NEG)
            attn = jax.nn.softmax(scores, axis=-1)
            return jnp.einsum('...nm,...md->...nd', attn, h) + b
        B, N, C = x.shape
        H, D, _ = Wh.shape
        mask = graph + jnp.eye(N, dtype=graph.dtype) > 0
        h = jnp.einsum('bnc,hdc->bhnd', x, Wh)
        out_h = _gat_layer(h, mask[None, None], bh[None, :, None, :])
        cat = jnp.transpose(out_h, (0, 2, 1, 3)).reshape(B, N, H * D)
        z = jax.nn.leaky_relu(cat, negative_slope=0.2)
        h2 = jnp.einsum('bnk,dk->bnd', z, Wo)
        out2 = _gat_layer(h2, mask[None], bo)
        z2 = jax.nn.leaky_relu(out2, negative_slope=0.2)
        mu = jnp.mean(z2, axis=-1, keepdims=True)
        var = jnp.mean(jnp.square(z2 - mu), axis=-1, keepdims=True)
        out = (z2 - mu) * jax.lax.rsqrt(var + LN_EPS) * gamma + beta
        return out

    def _L2_gnn_ref(X, A, weight, a):
        import jax, jax.numpy as jnp
        import numpy as np
        NEG_INF = -9000000000000000.0
        LEAKY_SLOPE = 0.01
        B, N, _ = X.shape
        Fout = weight.shape[1]
        mask = (A > 0) | jnp.eye(N, dtype=bool)
        Xw = jnp.matmul(X, weight)
        a_l = a[:Fout, 0]
        a_r = a[Fout:, 0]
        left = jnp.einsum('bnf,f->bn', Xw, a_l)
        right = jnp.einsum('bnf,f->bn', Xw, a_r)
        e = left[:, :, None] + right[:, None, :]
        e = jnp.where(e >= 0, e, LEAKY_SLOPE * e)
        att = jnp.where(mask[None, :, :], e, NEG_INF)
        att = jax.nn.softmax(att, axis=-1)
        out = jnp.matmul(att, Xw)
        return out

    def _L3_gnn_ref(x, adj, W, a):
        import jax, jax.numpy as jnp
        import numpy as np
        ALPHA = 0.2
        NEG_INF = -1e+30
        Dout = W.shape[1]
        h = jnp.einsum('bnd,de->bne', x, W)
        a1, a2 = (a[:Dout], a[Dout:])
        s_i = h @ a1
        s_j = h @ a2
        e = s_i[:, :, None] + s_j[:, None, :]
        e = jnp.where(e >= 0, e, ALPHA * e)
        e = jnp.where(adj[None, :, :] > 0, e, NEG_INF)
        attn = jax.nn.softmax(e, axis=-1)
        return jnp.einsum('bij,bjd->bid', attn, h)
    x = _layernorm(x + _L0_gnn_ref(x, L0_gnn_W, L0_gnn_a, adj), axis=-1)
    x = _layernorm(x + _L1_gnn_ref(x, adj, L1_gnn_Wh, L1_gnn_bh, L1_gnn_Wo, L1_gnn_bo, L1_gnn_gamma, L1_gnn_beta), axis=-1)
    x = _layernorm(x + _L2_gnn_ref(x, adj, L2_gnn_weight, L2_gnn_a), axis=-1)
    x = _layernorm(x + _L3_gnn_ref(x, adj, L3_gnn_W, L3_gnn_a), axis=-1)
    return x

_drawn_inputs = setup_inputs


def setup_inputs(seed=0):
    import zlib

    import numpy as np

    out = dict(_drawn_inputs(seed))
    spreads = {'L1_gnn_bh': (0.0, 0.1),
     'L1_gnn_bo': (0.0, 0.1),
     'L1_gnn_gamma': (1.0, 0.2),
     'L1_gnn_beta': (0.0, 0.1)}
    factors = {}
    for name, (base, spread) in spreads.items():
        noise = np.random.default_rng([zlib.crc32(name.encode()), seed]).standard_normal(out[name].shape)
        drawn = base * np.exp(spread * noise) if base else spread * noise
        out[name] = jnp.asarray(drawn.astype(out[name].dtype))
    for name, factor in factors.items():
        out[name] = (out[name] * factor).astype(out[name].dtype)
    return out
```

```python
import concourse.bass as bass
from concourse import mybir
from contextlib import ExitStack

F32 = mybir.dt.float32
F32R = mybir.dt.float32r
BF16 = mybir.dt.bfloat16
I32 = mybir.dt.int32
ALU = mybir.AluOpType
ACT = mybir.ActivationFunctionType
X_AXIS = mybir.AxisListType.X

B, N, D = 8, 2048, 64
P = 128
NB = N // P
H = 4
BANK = 512
NC = N // BANK
HALF = N // 2
MASKED = -1.0e30
EMPTY = -1.0e29
EPS = 1e-5
UNITS = 7
GATS = H + 1
ADDS = 2


def drain_link(eng):
    eng.drain()


def stand_alone_wait(eng, sem, value, gates):
    eng.wait_ge(sem, value)
    eng.sem_inc(gates, 1)


def layer_norm(nc, dve, pool_gate, x, sq, st, groups):
    start_pow, pow_done, value = pool_gate
    sums, var, rstd = st[:, 0, :], st[:, 1, :], st[:, 2, :]

    def spread(v):
        return v.unsqueeze(2).to_broadcast([P, groups, D])

    drain_link(dve)
    nc.vector.tensor_reduce(sums, x, axis=X_AXIS, op=ALU.add)
    drain_link(dve)
    nc.vector.scalar_tensor_tensor(out=x, in0=spread(sums), scalar=-1.0 / D, in1=x,
                                   op0=ALU.mult, op1=ALU.add)
    drain_link(dve)
    nc.vector.tensor_tensor(sq, x, x, ALU.mult)
    drain_link(dve)
    nc.vector.tensor_reduce(var, sq, axis=X_AXIS, op=ALU.add)
    drain_link(dve)
    nc.vector.tensor_scalar(var, var, 1.0 / D, EPS, ALU.mult, ALU.add).then_inc(start_pow, 1)
    dve.wait_ge(pow_done, value)
    return nc.vector.tensor_tensor(x, x, spread(rstd), ALU.mult)


def gated_sum_layer(nc, x, xt, adj, w, at, x1, mask, ident, half_power, diag, out_sem):
    BD = B * D
    PAIRS = B // 2
    JOUTER = 4
    ACCS = 5
    ctx = ExitStack()
    with ctx:
        def sb(name, shape, dt):
            return ctx.enter_context(nc.sbuf_tensor(name, shape, dt))

        def ps(name):
            return ctx.enter_context(nc.psum_tensor(name, [P, BANK], F32))

        def sem(name):
            return ctx.enter_context(nc.semaphore(name))

        xtp = sb("xtp", [P, PAIRS, N + 1], F32)
        w2 = sb("w2", [P, P], F32)
        hn = sb("hn", [P, NB, BD], F32)
        parts = sb("parts", [P, 3, NB, BD], BF16)
        rest = sb("rest", [P, 2, BD], F32)
        adjb = sb("adjb", [P, 2, HALF], I32)
        ones = sb("ones", [P, P], F32)
        hsum = sb("hsum", [P, BD], F32)
        ab = sb("ab", [P, 2, 2 * D], F32)
        xb = sb("xb0", [P, 2, BD], F32)
        t1 = sb("t1", [P, 2, BD], F32)
        t2 = sb("t2", [P, BD], F32)
        score = sb("score", [P, B], F32)
        st = sb("st0", [P, 3, B], F32)
        acc = [ps(f"acc{i}") for i in range(ACCS)]
        ph, pshift, psum = ps("ph"), ps("pshift"), ps("psum_h")

        adj_in = [sem(f"adj_in{i}") for i in range(2)]
        adj_used = sem("adj_used")
        xt_in = sem("xt_in")
        w_in = sem("w_in")
        cleared = sem("cleared")
        blk_in = [sem(f"blk_in{i}") for i in range(2)]
        blk_used = sem("blk_used")
        stored = [sem(f"stored{i}") for i in range(2)]
        h_ready = sem("h_ready")
        hs_ready = sem("hs_ready")
        hn_copied = sem("hn_copied")
        part1 = sem("part1")
        rest_ready = sem("rest_ready")
        parts_ready = sem("parts_ready")
        sum_ready = sem("sum_ready")
        sum_copied = sem("sum_copied")
        acc_ready = sem("acc_ready")
        acc_read = sem("acc_read")
        x1_ready = sem("x1_ready")
        var_ready = sem("var_ready0")
        pow_done = sem("pow_done0")
        id_ready = sem("id_ready")
        block = ctx.enter_context(nc.Block())

        xn = x.rearrange("b (k p) d -> p k b d", p=P)
        x1n = x1.rearrange("b (k p) d -> p k b d", p=P)

        @block.sync
        def _(sp):
            sp.wait_ge(cleared, 2)
            sp.dma_start(w2[0:D, 0:D], w).then_inc(w_in, 16)
            sp.dma_start(w2[D:P, D:P], w).then_inc(w_in, 16)
            for pair in range(PAIRS):
                sp.dma_start(xtp[:, pair, 2:], xt[pair, :, 1:]).then_inc(xt_in, 16)
            for k in range(NB):
                for half in range(2):
                    if k >= 1:
                        sp.wait_ge(adj_used, 2 * k + half - 1)
                    sp.dma_start(adjb[:, half, :], adj[k * P:(k + 1) * P, half * HALF:(half + 1) * HALF])\
                      .then_inc(adj_in[half], 16)

        @block.gpsimd
        def _(pool):
            nc.gpsimd.memset(w2[:], 0.0).then_inc(cleared, 1)
            nc.gpsimd.memset(xtp[:, :, 0:2], 0.0).then_inc(cleared, 1)
            nc.gpsimd.memset(ones[:], 1.0).then_inc(id_ready, 1)
            nc.gpsimd.memset(half_power[:], -0.5).then_inc(id_ready, 1)
            nc.gpsimd.memset(ident[:], 0.0).then_inc(id_ready, 1)
            pool.wait_ge(id_ready, 3)
            nc.gpsimd.affine_select(out=ident[:], in_=ident[:], compare_op=ALU.not_equal, fill=1.0,
                                    base=0, pattern=[[-1, P]], channel_multiplier=1).then_inc(id_ready, 1)
            for k in range(NB):
                pool.wait_ge(var_ready, k + 1)
                nc.gpsimd.tensor_tensor(st[:, 2, :], st[:, 1, :], half_power[:, 0:B],
                                        ALU.pow).then_inc(pow_done, 1)

        @block.tensor
        def _(pe):
            pe.wait_ge(w_in, 32)
            pe.wait_ge(xt_in, 16 * PAIRS)
            pe.wait_ge(id_ready, 4)
            for k in range(NB):
                if k >= 1:
                    pe.wait_ge(hn_copied, k)
                for pair in range(PAIRS):
                    last = nc.tensor.matmul(ph[:, pair * P:(pair + 1) * P],
                                            xtp[:, pair, 1 + k * P:1 + (k + 1) * P], w2[:],
                                            start=True, stop=True)
                last.then_inc(h_ready, 1)
                if k >= 1:
                    pe.wait_ge(rest_ready, k)
                for pair in range(PAIRS):
                    last = nc.tensor.matmul(pshift[:, pair * P:(pair + 1) * P],
                                            xtp[:, pair, k * P:(k + 1) * P], w2[:],
                                            start=True, stop=True)
                last.then_inc(hs_ready, 1)
                pe.wait_ge(hn_copied, k + 1)
                last = nc.tensor.matmul(psum[:], ones[:], hn[:, k, :], start=(k == 0), stop=(k == NB - 1))
            last.then_inc(sum_ready, 1)
            for j in range(NB):
                pe.wait_ge(adj_used, 2 * j + 2)
                pe.wait_ge(parts_ready, j + 1)
                for i in range(JOUTER):
                    for part in range(3):
                        last = nc.tensor.matmul(acc[i][:], mask[:, j, i * P:(i + 1) * P],
                                                parts[:, part, j, :], start=(j == 0 and part == 0),
                                                stop=(j == NB - 1 and part == 2))
                    if j == NB - 1:
                        last.then_inc(acc_ready, 1)
            for i in range(JOUTER, NB):
                if i >= ACCS:
                    pe.wait_ge(acc_read, i - ACCS + 1)
                for j in range(NB):
                    for part in range(3):
                        last = nc.tensor.matmul(acc[i % ACCS][:], mask[:, j, i * P:(i + 1) * P],
                                                parts[:, part, j, :], start=(j == 0 and part == 0),
                                                stop=(j == NB - 1 and part == 2))
                last.then_inc(acc_ready, 1)

        @block.scalar
        def _(act):
            for k in range(2):
                act.dma_start(xb[:, k, :].rearrange("p (b d) -> p b d", b=B), xn[:, k]).then_inc(blk_in[k], 16)
                act.dma_start(ab[:, k, :], at[k * P:(k + 1) * P, :]).then_inc(blk_in[k], 16)
            for k in range(NB):
                act.wait_ge(h_ready, k + 1)
                nc.scalar.copy(hn[:, k, :], ph[:]).then_inc(hn_copied, 1)
                act.wait_ge(hs_ready, k + 1)
                nc.scalar.copy(parts[:, 0, k, :], pshift[:]).then_inc(part1, 1)
            act.wait_ge(sum_ready, 1)
            nc.scalar.copy(hsum[:], psum[:]).then_inc(sum_copied, 1)
            for k in range(NB):
                act.wait_ge(x1_ready, k + 1)
                act.dma_start(x1n[:, k], t1[:, k % 2, :].rearrange("p (b d) -> p b d", b=B))\
                   .then_inc(stored[k % 2], 16)
                if k + 2 < NB:
                    act.wait_ge(blk_used, k + 1)
                    act.dma_start(xb[:, k % 2, :].rearrange("p (b d) -> p b d", b=B), xn[:, k + 2])\
                       .then_inc(blk_in[k % 2], 16)
                    act.dma_start(ab[:, k % 2, :], at[(k + 2) * P:(k + 3) * P, :]).then_inc(blk_in[k % 2], 16)
            for s in stored:
                act.wait_ge(s, 16 * NB // 2)

        @block.vector
        def _(dve):
            for k in range(NB):
                for half in range(2):
                    dve.wait_ge(adj_in[half], 16 * (k + 1))
                    nc.vector.tensor_scalar(mask[:, k, half * HALF:(half + 1) * HALF], adjb[:, half, :], 0,
                                            None, ALU.is_gt).then_inc(adj_used, 1)
                dve.wait_ge(part1, k + 1)
                r = rest[:, k % 2, :]
                nc.vector.tensor_tensor(r, pshift[:], parts[:, 0, k, :], ALU.subtract).then_inc(rest_ready, 1)
                drain_link(dve)
                nc.vector.tensor_copy(parts[:, 1, k, :], r)
                drain_link(dve)
                nc.vector.tensor_tensor(parts[:, 2, k, :], r, parts[:, 1, k, :], ALU.subtract)\
                  .then_inc(parts_ready, 1)
            dve.wait_ge(sum_copied, 1)
            for i in range(NB):
                t = t1[:, i % 2, :]
                t3 = t.rearrange("p (b d) -> p b d", b=B)
                dve.wait_ge(blk_in[i % 2], 32 * (i // 2 + 1))
                if i >= 2:
                    dve.wait_ge(stored[i % 2], 16 * (i // 2))
                a1 = ab[:, i % 2, 0:D].unsqueeze(1).to_broadcast([P, B, D])
                a2 = ab[:, i % 2, D:2 * D].unsqueeze(1).to_broadcast([P, B, D])
                drain_link(dve)
                nc.vector.tensor_tensor(t3, hn[:, i, :].rearrange("p (b d) -> p b d", b=B), a1, ALU.mult)
                dve.wait_ge(acc_ready, i + 1)
                nc.vector.tensor_tensor(t2[:].rearrange("p (b d) -> p b d", b=B),
                                        acc[i % ACCS][:].rearrange("p (b d) -> p b d", b=B), a2,
                                        ALU.mult).then_inc(acc_read, 1)
                drain_link(dve)
                nc.vector.tensor_tensor(t, t, t2[:], ALU.add)
                drain_link(dve)
                nc.vector.tensor_reduce(score[:], t3, axis=X_AXIS, op=ALU.add)
                drain_link(dve)
                if i == 0:
                    nc.vector.memset(score[0:1, :], 0.0)
                    drain_link(dve)
                nc.vector.tensor_tensor(t3, hsum[:].rearrange("p (b d) -> p b d", b=B),
                                        score[:].unsqueeze(2).to_broadcast([P, B, D]), ALU.mult)
                drain_link(dve)
                nc.vector.scalar_tensor_tensor(out=t, in0=t, scalar=0.2, in1=t, op0=ALU.mult, op1=ALU.max)
                drain_link(dve)
                nc.vector.tensor_tensor(t, t, xb[:, i % 2, :], ALU.add).then_inc(blk_used, 1)
                layer_norm(nc, dve, (var_ready, pow_done, i + 1), t3,
                           t2[:].rearrange("p (b d) -> p b d", b=B), st, B).then_inc(x1_ready, 1)
            for k in range(NB):
                nc.vector.tensor_scalar(mask[:, k, :], mask[:, k, :], -1.0, -MASKED, ALU.add, ALU.mult)
            drain_link(dve)
            dblocks = diagonal_blocks(mask)
            nc.vector.tensor_tensor(diag[:], dblocks, ident[:].unsqueeze(1).to_broadcast([P, NB, P]), ALU.mult)
            drain_link(dve)
            nc.vector.tensor_tensor(dblocks, dblocks, diag[:], ALU.subtract)


def diagonal_blocks(mask):
    return bass.AP(mask[:].tensor, 0, [[NB * N, P], [N + P, NB], [1, P]])


def attention_layers(nc, x1, out, whd, bh, wod, bo, gamma, beta, w2, a2, w3, a3,
                     mask, ident, half_power, diag):
    ctx = ExitStack()
    with ctx:
        def sb(name, shape, dt):
            return ctx.enter_context(nc.sbuf_tensor(name, shape, dt))

        def sem(name):
            return ctx.enter_context(nc.semaphore(name))

        xb = sb("xb", [P, NB, D], F32)
        y = sb("y", [P, NB, D], F32)
        tmp = sb("tmp", [P, NB, D], F32)
        st = sb("st", [P, 3, NB], F32)
        wide = sb("wide", [P, 4, N], F32)
        xt = wide[0:D, 0, :]
        zt = wide[:, 0:2, :]
        z = sb("z", [P, NB, H * D], F32)
        zf = z[:].rearrange("p k n -> p (k n)")
        rr = zf[:, 0:N]
        sr = zf[:, N:2 * N]
        r1 = sb("r1", [P, N], F32R)
        r2 = sb("r2", [P, N], F32R)
        lt = sb("lt", [P, N], F32R)
        hn = sb("hn1", [P, NB, D + 1], F32)
        sm = sb("sm", [P, 2, N], F32)
        pt = sb("pt", [P, 2, N], F32)
        mx = sb("mx", [P, NB, 2], F32)
        rc = sb("rc", [P, NB], F32)
        wc = sb("wc", [D, 2 * D], F32)
        wo = sb("wo", [P, 2, 2 * D], F32)
        wl = sb("wl", [D, ADDS, D], F32)
        av = sb("av", [P, ADDS, 2, D], F32)
        bhs = sb("bhs", [P, H, D], F32)
        bos = sb("bos", [P, D], F32)
        gam = sb("gam", [P, D], F32)
        bet = sb("bet", [P, D], F32)
        left = sb("left", [P, NB], F32)
        right = sb("right", [P, NB], F32)
        rm = sb("rm", [P, NB], F32)
        ev = sb("ev", [P, NB], F32)
        mv = sb("mv", [P, NB], F32)
        avv = sb("avv", [P, NB], F32)
        bvv = sb("bvv", [P, NB], F32)
        fv = sb("fv", [P, NB], F32)
        hs = sb("hs", [P, D + 1], F32)
        o1 = sb("o1", [P, D + 1], F32)
        ones = sb("ones1", [P, P], F32)

        pss = ctx.enter_context(nc.psum_tensor("pss", [P, N], F32))
        tp = [ctx.enter_context(nc.psum_tensor(f"tp{i}", [P, BANK], F32)) for i in range(3)]
        po = ctx.enter_context(nc.psum_tensor("po", [P, BANK], F32))

        gates = sem("gates")
        const_in = sem("const_in")
        ones_set = sem("ones_set")
        x_in = sem("x_in")
        x_out = sem("x_out")
        wc_in = sem("wc_in")
        xt_psum = sem("xt_psum")
        xt_ready = sem("xt_ready")
        x_ready = sem("x_ready")
        proj_ready = sem("proj_ready")
        r1_ready = sem("r1_ready")
        r2_ready = sem("r2_ready")
        lt_ready = sem("lt_ready")
        hn_psum = sem("hn_psum")
        hn_ready = sem("hn_ready")
        scores_ready = sem("scores_ready")
        scores_read = sem("scores_read")
        rows_ready = sem("rows_ready")
        tr_ready = sem("tr_ready")
        exp_ready = sem("exp_ready")
        pv_ready = sem("pv_ready")
        out_read = sem("out_read")
        z_ready = sem("z_ready")
        zt_psum = sem("zt_psum")
        zt_ready = sem("zt_ready")
        right_ready = sem("right_ready")
        right_psum = sem("right_psum")
        right_copied = sem("right_copied")
        hs_psum = sem("hs_psum")
        diag_closed = sem("diag_closed")
        var_ready = sem("var_ready")
        pow_done = sem("pow_done")
        block = ctx.enter_context(nc.Block())

        LNS = 4
        CONSTS = 8

        @block.sync
        def _(sp):
            sp.dma_start(wo[:], wod.rearrange("(k p) n -> p k n", p=P)).then_inc(const_in, 16)
            sp.dma_start(wl[:, 0, :], w2).then_inc(const_in, 16)
            sp.dma_start(wl[:, 1, :], w3).then_inc(const_in, 16)
            sp.dma_start(av[:, 0], a2.rearrange("(o s d) -> o s d", o=1, s=2).to_broadcast([P, 2, D]))\
              .then_inc(const_in, 16)
            sp.dma_start(av[:, 1], a3.rearrange("(o s d) -> o s d", o=1, s=2).to_broadcast([P, 2, D]))\
              .then_inc(const_in, 16)
            sp.dma_start(bhs[:], bh.rearrange("(o h) d -> o h d", o=1).to_broadcast([P, H, D]))\
              .then_inc(const_in, 16)
            for tile, src in ((bos, bo), (gam, gamma), (bet, beta)):
                sp.dma_start(tile[:], src.rearrange("(o d) -> o d", o=1).to_broadcast([P, D]))\
                  .then_inc(const_in, 16)
            with sp.Fori(0, B) as b:
                sp.dma_start(xb[:], x1[bass.ds(b, 1)].rearrange("o (k p) d -> p (o k) d", p=P))\
                  .then_inc(x_in, 16)
                with sp.Fori(0, H) as h:
                    sp.dma_start(wc[:], whd[bass.ds(h, 1)].rearrange("o c n -> (o c) n")).then_inc(wc_in, 16)
                    stand_alone_wait(sp, hn_psum, b * (2 * UNITS) + h * 2 + 2, gates)
                stand_alone_wait(sp, x_ready, b * 3 + 3, gates)
                sp.dma_start(out[bass.ds(b, 1)].rearrange("o (k p) d -> p (o k) d", p=P), xb[:])\
                  .then_inc(x_out, 16)
                stand_alone_wait(sp, x_out, b * 16 + 16, gates)
            sp.wait_ge(x_out, B * 16)

        @block.gpsimd
        def _(pool):
            nc.gpsimd.memset(hn[:, :, D:D + 1], 1.0).then_inc(ones_set, 1)
            nc.gpsimd.memset(ones[:], 1.0).then_inc(ones_set, 1)
            with pool.Fori(0, B) as b:
                for n in range(LNS):
                    stand_alone_wait(pool, var_ready, b * LNS + n + 1, gates)
                    nc.gpsimd.tensor_tensor(st[:, 2, :], st[:, 1, :], half_power[:, 0:NB],
                                            ALU.pow).then_inc(pow_done, 1)

        @block.tensor
        def _(pe):
            def transpose_x():
                for c in range(NC):
                    for q in range(4):
                        k = c * 4 + q
                        last = nc.tensor.transpose(pss[0:D, k * P:(k + 1) * P], xb[:, k, :], ident[:])
                    last.then_inc(xt_psum, 1)

            def project_nodes(w, chunks, unit):
                for half in range(2):
                    for q in range(NB // 2):
                        k = half * (NB // 2) + q
                        terms = chunks(k, w)
                        for ci, (lhs, rhs) in enumerate(terms):
                            last = nc.tensor.matmul(tp[half][:, q * D:(q + 1) * D], lhs, rhs,
                                                    start=(ci == 0), stop=(ci == len(terms) - 1))
                    last.then_inc(hn_psum, 1)

            def transpose_tile(t, q, unit, sources):
                k = 4 * t + q
                if k >= 3:
                    stand_alone_wait(pe, exp_ready, unit * 64 + (k - 2), gates)
                for s in range(4):
                    jb = 4 * q + s
                    for n, src in enumerate(sources):
                        last = nc.tensor.matmul(tp[k % 3][:, s * P:(s + 1) * P],
                                                src[:, jb * P:(jb + 1) * P], ident[:],
                                                is_transpose=True, start=(n == 0),
                                                stop=(n == len(sources) - 1))
                last.then_inc(tr_ready, 1)

            def weighted_sum(t, unit):
                stand_alone_wait(pe, exp_ready, unit * 64 + 4 * (t + 1), gates)
                if t >= 1:
                    stand_alone_wait(pe, out_read, unit * NB + t, gates)
                for jb in range(NB):
                    last = nc.tensor.matmul(po[:, 0:D + 1], pt[:, t % 2, jb * P:(jb + 1) * P], hn[:, jb, :],
                                            start=(jb == 0), stop=(jb == NB - 1))
                last.then_inc(pv_ready, 1)

            def gat_unit(unit, g):
                stand_alone_wait(pe, r2_ready, g * NC + NC, gates)
                stand_alone_wait(pe, lt_ready, g * 2 + 2, gates)
                stand_alone_wait(pe, hn_ready, unit * 2 + 2, gates)
                for t in range(NB + 2):
                    if t < NB:
                        for half in range(2):
                            if t >= 1:
                                stand_alone_wait(pe, scores_read, g * 2 * NB + (2 * (t - 1) + half + 1), gates)
                            for c in range(half * NC // 2, (half + 1) * NC // 2):
                                cols = slice(c * BANK, (c + 1) * BANK)
                                lhs = lt[:, t * P:(t + 1) * P]
                                nc.tensor.matmul(pss[:, cols], lhs, r1[:, cols], start=True, stop=False)
                                last = nc.tensor.matmul(pss[:, cols], lhs, r2[:, cols], start=False, stop=True)
                            last.then_inc(scores_ready, 1)
                    if 1 <= t <= NB:
                        stand_alone_wait(pe, rows_ready, unit * NB + t, gates)
                        for q in range(4):
                            transpose_tile(t - 1, q, unit, [sm[:, (t - 1) % 2, :]])
                    if t >= 2:
                        weighted_sum(t - 2, unit)

            def add_unit(unit, v, k, xt_count):
                transpose_x()
                stand_alone_wait(pe, xt_ready, xt_count, gates)
                project_nodes(wl[:, k, :], lambda n, w: [(xt[:, n * P:(n + 1) * P], w)], unit)
                stand_alone_wait(pe, right_ready, v + 1, gates)
                for n in range(NB):
                    last = nc.tensor.transpose(pss[:, n * P:(n + 1) * P],
                                               right[:, n:n + 1].to_broadcast([P, P]), ident[:])
                last.then_inc(right_psum, 1)
                if k == 1:
                    for n in range(NB):
                        last = nc.tensor.matmul(po[:, 0:D + 1], ones[:], hn[:, n, :], start=(n == 0),
                                                stop=(n == NB - 1))
                    last.then_inc(hs_psum, 1)
                for t in range(NB + 1):
                    if t < NB:
                        stand_alone_wait(pe, rows_ready, unit * NB + t + 1, gates)
                        for q in range(4):
                            transpose_tile(t, q, unit, [sm[:, t % 2, :], wide[:, t % 4, :]])
                    if t >= 1:
                        weighted_sum(t - 1, unit)

            pe.wait_ge(const_in, 16 * (CONSTS + 1))
            pe.wait_ge(ones_set, 2)
            with pe.Fori(0, B) as b:
                stand_alone_wait(pe, x_in, b * 16 + 16, gates)
                transpose_x()
                stand_alone_wait(pe, xt_ready, b * 3 * NC + NC, gates)
                with pe.Fori(0, H) as h:
                    stand_alone_wait(pe, wc_in, b * H * 16 + h * 16 + 16, gates)
                    for c in range(NC):
                        cols = slice(c * BANK, (c + 1) * BANK)
                        nc.tensor.matmul(pss[:, cols], wc[:], xt[:, cols], start=True, stop=True)\
                          .then_inc(proj_ready, 1)
                    project_nodes(wc[:, 0:D], lambda n, w: [(xt[:, n * P:(n + 1) * P], w)], None)
                    gat_unit(b * UNITS + h, b * GATS + h)
                stand_alone_wait(pe, z_ready, b * H + H, gates)
                for n in range(8):
                    if n >= 3:
                        stand_alone_wait(pe, zt_ready, b * 8 + (n - 2), gates)
                    for q in range(4):
                        k = (n % 4) * 4 + q
                        last = nc.tensor.transpose(tp[n % 3][:, q * P:(q + 1) * P],
                                                   z[:, k, (n // 4) * P:(n // 4 + 1) * P], ident[:])
                    last.then_inc(zt_psum, 1)
                stand_alone_wait(pe, zt_ready, b * 8 + 8, gates)
                for c in range(NC):
                    cols = slice(c * BANK, (c + 1) * BANK)
                    for ci in range(2):
                        last = nc.tensor.matmul(pss[:, cols], wo[:, ci, :], zt[:, ci, cols],
                                                start=(ci == 0), stop=(ci == 1))
                    last.then_inc(proj_ready, 1)
                project_nodes(None, lambda n, w: [(zt[:, ci, n * P:(n + 1) * P], wo[:, ci, 0:D])
                                                  for ci in range(2)], None)
                gat_unit(b * UNITS + H, b * GATS + H)
                for k in range(ADDS):
                    stand_alone_wait(pe, x_ready, b * 3 + k + 1, gates)
                    add_unit(b * UNITS + GATS + k, b * ADDS + k, k, b * (3 * NC) + (k + 2) * NC)

        @block.scalar
        def _(act):
            def copy_xt(n):
                for c in range(NC):
                    stand_alone_wait(act, xt_psum, n * NC + c + 1, gates)
                    nc.scalar.copy(xt[:, c * BANK:(c + 1) * BANK], pss[0:D, c * BANK:(c + 1) * BANK])\
                      .then_inc(xt_ready, 1)

            def copy_hn(unit):
                for half in range(2):
                    stand_alone_wait(act, hn_psum, unit * 2 + half + 1, gates)
                    nc.scalar.copy(hn[:, half * NB // 2:(half + 1) * NB // 2, 0:D],
                                   tp[half][:].rearrange("p (k d) -> p k d", d=D)).then_inc(hn_ready, 1)

            def exps(unit):
                for t in range(NB):
                    if t >= 2:
                        stand_alone_wait(act, pv_ready, unit * NB + (t - 1), gates)
                    for q in range(4):
                        k = 4 * t + q
                        stand_alone_wait(act, tr_ready, unit * 64 + k + 1, gates)
                        nc.scalar.activation(pt[:, t % 2, q * BANK:(q + 1) * BANK], tp[k % 3][:], ACT.Exp)\
                          .then_inc(exp_ready, 1)

            def gat_unit(unit, g):
                for c in range(NC):
                    cols = slice(c * BANK, (c + 1) * BANK)
                    stand_alone_wait(act, proj_ready, g * NC + c + 1, gates)
                    nc.scalar.copy(r1[:, cols], pss[:, cols]).then_inc(r1_ready, 1)
                copy_hn(unit)
                stand_alone_wait(act, r1_ready, g * NC + NC, gates)
                nc.scalar.copy(lt[0:D, :], r1[0:D, :].bitcast(F32)).then_inc(lt_ready, 1)
                exps(unit)

            with act.Fori(0, B) as b:
                copy_xt(b * 3)
                with act.Fori(0, H) as h:
                    gat_unit(b * UNITS + h, b * GATS + h)
                for n in range(8):
                    stand_alone_wait(act, zt_psum, b * 8 + n + 1, gates)
                    nc.scalar.copy(zt[:, n // 4, (n % 4) * BANK:(n % 4 + 1) * BANK], tp[n % 3][:])\
                      .then_inc(zt_ready, 1)
                gat_unit(b * UNITS + H, b * GATS + H)
                for k, slope in enumerate((0.01, 0.2)):
                    copy_xt(b * 3 + k + 1)
                    copy_hn(b * UNITS + GATS + k)
                    stand_alone_wait(act, right_psum, b * ADDS + k + 1, gates)
                    nc.scalar.mul(sr, pss[:], slope).then_inc(right_copied, 1)
                    nc.scalar.mul(rr, pss[:], 1.0 - slope).then_inc(right_copied, 1)
                    exps(b * UNITS + GATS + k)

        @block.vector
        def _(dve):
            def normalise(t, unit, bias, dest):
                stand_alone_wait(dve, pv_ready, unit * NB + t + 1, gates)
                nc.vector.reciprocal(rc[:, t:t + 1], po[:, D:D + 1])
                drain_link(dve)
                nc.vector.scalar_tensor_tensor(out=dest, in0=po[:, 0:D], scalar=rc[:, t:t + 1], in1=bias,
                                               op0=ALU.mult, op1=ALU.add).then_inc(out_read, 1)

            def gat_unit(unit, g, bias):
                for c in range(NC):
                    cols = slice(c * BANK, (c + 1) * BANK)
                    stand_alone_wait(dve, r1_ready, g * NC + c + 1, gates)
                    nc.vector.tensor_tensor(r2[:, cols], pss[:, cols], r1[:, cols].bitcast(F32),
                                            ALU.subtract).then_inc(r2_ready, 1)
                drain_link(dve)
                nc.vector.tensor_copy(lt[D:P, :], r2[D:P, :].bitcast(F32)).then_inc(lt_ready, 1)
                for t in range(NB + 2):
                    if t < NB:
                        if t >= 2:
                            stand_alone_wait(dve, tr_ready, unit * 64 + 4 * (t - 1), gates)
                        for half in range(2):
                            cols = slice(half * HALF, (half + 1) * HALF)
                            stand_alone_wait(dve, scores_ready, g * 2 * NB + (2 * t + half + 1), gates)
                            nc.vector.tensor_tensor_reduce(
                                out=sm[:, t % 2, cols], in0=pss[:, cols], in1=mask[:, t, cols], scale=1.0,
                                scalar=(2 * MASKED if half == 0 else mx[:, t, 0:1]), op0=ALU.add, op1=ALU.max,
                                accum_out=mx[:, t, half:half + 1]).then_inc(scores_read, 1)
                            drain_link(dve)
                        nc.vector.tensor_scalar(sm[:, t % 2, :], sm[:, t % 2, :], mx[:, t, 1:2], None,
                                                ALU.subtract).then_inc(rows_ready, 1)
                    if t >= 2:
                        normalise(t - 2, unit, bias, y[:, t - 2, :])
                drain_link(dve)

            def add_unit(unit, v, k, slope):
                stand_alone_wait(dve, hn_ready, unit * 2 + 2, gates)
                for side, dest in ((0, left), (1, right)):
                    nc.vector.tensor_tensor(tmp[:], hn[:, :, 0:D],
                                            av[:, k, side:side + 1, :].to_broadcast([P, NB, D]), ALU.mult)
                    drain_link(dve)
                    last = nc.vector.tensor_reduce(dest[:], tmp[:], axis=X_AXIS, op=ALU.add)
                    drain_link(dve) if side == 0 else last.then_inc(right_ready, 1)
                stand_alone_wait(dve, right_copied, v * 2 + 2, gates)
                if k == 1:
                    nc.vector.tensor_tensor(diagonal_blocks(mask), diagonal_blocks(mask), diag[:], ALU.add)
                    stand_alone_wait(dve, hs_psum, b + 1, gates)
                    nc.vector.tensor_copy(hs[:], po[:, 0:D + 1]).then_inc(diag_closed, 1)
                    drain_link(dve)
                for t in range(NB + 2):
                    if t < NB and t % 2 == 0:
                        pair = slice(t, t + 2)
                        for u in (t, t + 1):
                            if u >= 4:
                                stand_alone_wait(dve, tr_ready, unit * 64 + 4 * (u - 3), gates)
                            nc.vector.tensor_tensor_reduce(
                                out=wide[:, u % 4, :], in0=sr, in1=mask[:, u, :], scale=1.0,
                                scalar=2 * MASKED, op0=ALU.add, op1=ALU.max, accum_out=rm[:, u:u + 1])
                        drain_link(dve)
                        nc.vector.scalar_tensor_tensor(out=ev[:, pair], in0=rm[:, pair], scalar=1.0 / slope,
                                                       in1=left[:, pair], op0=ALU.mult, op1=ALU.add)
                        drain_link(dve)
                        nc.vector.scalar_tensor_tensor(out=mv[:, pair], in0=ev[:, pair], scalar=slope,
                                                       in1=ev[:, pair], op0=ALU.mult, op1=ALU.max)
                        nc.vector.tensor_scalar(fv[:, pair], ev[:, pair], EMPTY, None, ALU.is_lt)
                        drain_link(dve)
                        nc.vector.tensor_scalar(mv[:, pair], mv[:, pair], EMPTY / 10, None, ALU.max)
                        drain_link(dve)
                        nc.vector.tensor_tensor(avv[:, pair], left[:, pair], mv[:, pair], ALU.subtract)
                        nc.vector.scalar_tensor_tensor(out=bvv[:, pair], in0=left[:, pair], scalar=slope,
                                                       in1=mv[:, pair], op0=ALU.mult, op1=ALU.subtract)
                        drain_link(dve)
                        for u in (t, t + 1):
                            if u >= 2:
                                stand_alone_wait(dve, tr_ready, unit * 64 + 4 * (u - 1), gates)
                            nc.vector.tensor_scalar(sm[:, u % 2, :], rr, avv[:, u:u + 1], bvv[:, u:u + 1],
                                                    ALU.add, ALU.max).then_inc(rows_ready, 1)
                    if t >= 2:
                        u = t - 2
                        stand_alone_wait(dve, pv_ready, unit * NB + u + 1, gates)
                        if k == 1:
                            nc.vector.scalar_tensor_tensor(out=o1[:], in0=hs[:], scalar=fv[:, u:u + 1],
                                                           in1=po[:, 0:D + 1], op0=ALU.mult,
                                                           op1=ALU.add).then_inc(out_read, 1)
                            drain_link(dve)
                            nc.vector.reciprocal(rc[:, u:u + 1], o1[:, D:D + 1])
                            drain_link(dve)
                            nc.vector.tensor_scalar(y[:, u, :], o1[:, 0:D], rc[:, u:u + 1], None, ALU.mult)
                            drain_link(dve)
                        else:
                            nc.vector.reciprocal(rc[:, u:u + 1], po[:, D:D + 1])
                            drain_link(dve)
                            nc.vector.tensor_scalar(y[:, u, :], po[:, 0:D], rc[:, u:u + 1], None, ALU.mult)\
                              .then_inc(out_read, 1)
                drain_link(dve)
                if k == 1:
                    nc.vector.tensor_tensor(diagonal_blocks(mask), diagonal_blocks(mask), diag[:], ALU.subtract)
                nc.vector.tensor_tensor(xb[:], xb[:], y[:], ALU.add)
                layer_norm(nc, dve, (var_ready, pow_done, b * LNS + 3 + k), xb[:], tmp[:], st, NB)\
                    .then_inc(x_ready, 1)

            def spread(v):
                return v[:].unsqueeze(1).to_broadcast([P, NB, D])

            dve.wait_ge(const_in, 16 * (CONSTS + 1))
            dve.wait_ge(ones_set, 2)
            with dve.Fori(0, B) as b:
                with dve.Fori(0, H) as h:
                    gat_unit(b * UNITS + h, b * GATS + h,
                             bhs[:, bass.ds(h, 1), :].rearrange("p o d -> p (o d)"))
                    nc.vector.scalar_tensor_tensor(out=z[:, :, bass.ds(h * D, D)], in0=y[:], scalar=0.2,
                                                   in1=y[:], op0=ALU.mult, op1=ALU.max).then_inc(z_ready, 1)
                    drain_link(dve)
                gat_unit(b * UNITS + H, b * GATS + H, bos[:])
                nc.vector.scalar_tensor_tensor(out=y[:], in0=y[:], scalar=0.2, in1=y[:], op0=ALU.mult,
                                               op1=ALU.max)
                layer_norm(nc, dve, (var_ready, pow_done, b * LNS + 1), y[:], tmp[:], st, NB)
                drain_link(dve)
                nc.vector.tensor_tensor(y[:], y[:], spread(gam), ALU.mult)
                drain_link(dve)
                nc.vector.tensor_tensor(y[:], y[:], spread(bet), ALU.add)
                drain_link(dve)
                stand_alone_wait(dve, x_in, b * 16 + 16, gates)
                nc.vector.tensor_tensor(xb[:], xb[:], y[:], ALU.add)
                layer_norm(nc, dve, (var_ready, pow_done, b * LNS + 2), xb[:], tmp[:], st, NB)\
                    .then_inc(x_ready, 1)
                for k, slope in enumerate((0.01, 0.2)):
                    add_unit(b * UNITS + GATS + k, b * ADDS + k, k, slope)


def build(nc, x, xt, adj, w0, a0, whd, bh, wod, bo, gamma, beta, w2, a2, w3, a3, out):
    x1 = nc.dram_tensor("x1", [B, N, D], F32).ap()
    with ExitStack() as ctx:
        mask = ctx.enter_context(nc.sbuf_tensor("mask", [P, NB, N], BF16))
        diag = ctx.enter_context(nc.sbuf_tensor("diag", [P, NB, P], BF16))
        ident = ctx.enter_context(nc.sbuf_tensor("ident", [P, P], F32))
        half_power = ctx.enter_context(nc.sbuf_tensor("half_power", [P, NB], F32))
        gated_sum_layer(nc, x, xt, adj, w0, a0, x1, mask, ident, half_power, diag, None)
        attention_layers(nc, x1, out, whd, bh, wod, bo, gamma, beta, w2, a2, w3, a3,
                         mask, ident, half_power, diag)


def kernel(x, adj, L0_gnn_W, L0_gnn_a, L1_gnn_Wh, L1_gnn_bh, L1_gnn_Wo, L1_gnn_bo, L1_gnn_gamma,
           L1_gnn_beta, L2_gnn_weight, L2_gnn_a, L3_gnn_W, L3_gnn_a):
    import numpy as np
    import concourse.bacc as bacc
    from concourse.bass_utils import run_bass_kernel_spmd as run

    def c(v):
        return np.ascontiguousarray(v)

    x = np.asarray(x)
    wh = np.asarray(L1_gnn_Wh).transpose(0, 2, 1)
    wo = np.asarray(L1_gnn_Wo).T
    arrays = {
        "x": c(x),
        "xt": c(x.transpose(0, 2, 1).reshape(B // 2, 2 * D, N)),
        "adj": c(adj),
        "w0": c(L0_gnn_W),
        "a0": c(np.asarray(L0_gnn_a).T),
        "whd": c(np.concatenate([wh, wh], axis=2)),
        "bh": c(L1_gnn_bh),
        "wod": c(np.concatenate([wo, wo], axis=1)),
        "bo": c(L1_gnn_bo),
        "gamma": c(L1_gnn_gamma),
        "beta": c(L1_gnn_beta),
        "w2": c(L2_gnn_weight),
        "a2": c(np.asarray(L2_gnn_a).reshape(-1)),
        "w3": c(L3_gnn_W),
        "a3": c(L3_gnn_a),
    }
    nc = bacc.Bacc("TRN2", target_bir_lowering=False, num_devices=1)
    args = [nc.dram_tensor(f"in_{n}", a.shape, mybir.dt.from_np(a.dtype), kind="ExternalInput").ap()
            for n, a in arrays.items()]
    out = nc.dram_tensor("out_0", [B, N, D], F32, kind="ExternalOutput").ap()
    build(nc, *args, out)
    r = run(nc, [{f"in_{n}": a for n, a in arrays.items()}], core_ids=[0])
    return r.results[0]["out_0"]
```

```python
import concourse.bass as bass
from concourse import mybir
from contextlib import ExitStack

F32 = mybir.dt.float32
F32R = mybir.dt.float32r
BF16 = mybir.dt.bfloat16
I32 = mybir.dt.int32
ALU = mybir.AluOpType
ACT = mybir.ActivationFunctionType
X_AXIS = mybir.AxisListType.X

B, N, D = 8, 2048, 64
P = 128
NB = N // P
H = 4
BANK = 512
NC = N // BANK
HALF = N // 2
MASKED = -1.0e30
EMPTY = -1.0e29
EPS = 1e-5
UNITS = 7
GAT2, ADD1, ADD2 = H, H + 1, H + 2
SLOPES = {ADD1: 0.01, ADD2: 0.2}
CH = NB // NC
RING = 3
STEPS = NB + 2


def side_tasks():
    side = []
    for u in range(UNITS):
        tasks = []
        for c in range(NC):
            done = CH * c + CH + 2
            if u < H - 1:
                tasks += [(2 + 2 * c, "proj", c), (3 + 2 * c, "hn", c)]
            elif u == H - 1:
                tasks += [(done + n, name, c) for n, name in enumerate(("z0", "z1", "proj", "hn"))]
            elif u == GAT2:
                tasks += [(done + n, name, c) for n, name in enumerate(("lna", "lnb", "lnc", "xt", "h", "r"))]
            elif u == ADD1:
                tasks += [(done + n, name, c) for n, name in enumerate(("ra", "rb", "xt", "h"))]
                tasks += [(STEPS + 2 * CH + c, "r", c)]
            else:
                tasks += [(done, "ra", c), (done + 1, "rb", c)]
                tasks += [(2 + 3 * c, "xn", c), (3 + 3 * c, "proj", c), (4 + 3 * c, "hn", c)]
        side.append(sorted(tasks, key=lambda x: x[0]))
    return side


SIDE = side_tasks()
GROUPS = (tuple(range(H)), (GAT2,), (ADD1,), (ADD2,))


def tasks_at(units, step):
    last = (len(units) - 1) * NB
    return [(u, name, c) for n, u in enumerate(units) for s, name, c in SIDE[u]
            if n * NB + s == step or (step is None and n * NB + s >= last + STEPS)]


def next_gat(unit):
    return 0 if unit == ADD2 else unit + 1


class Count:

    def __init__(self, sem, each):
        self.sem, self.each, self.n, self.batch = sem, each, 0, None

    def value(self, n=None):
        n = self.n if n is None else n
        return n if self.batch is None else self.batch * self.each + n


def enter_loop(counts, b):
    for c in counts:
        c.batch, c.start = b, c.n


def leave_loop(counts):
    for c in counts:
        assert c.n - c.start == c.each, (c.sem, c.n - c.start, c.each)


def drain_link(eng):
    eng.drain()


def stand_alone_wait(eng, sem, value, gates):
    eng.wait_ge(sem, value)
    eng.sem_inc(gates, 1)


def norm_start(nc, dve, x, sq, sums, var, groups, var_ready):
    drain_link(dve)
    nc.vector.tensor_reduce(sums, x, axis=X_AXIS, op=ALU.add)
    drain_link(dve)
    nc.vector.scalar_tensor_tensor(out=x, in0=spread(sums, groups), scalar=-1.0 / D, in1=x,
                                   op0=ALU.mult, op1=ALU.add)
    drain_link(dve)
    nc.vector.tensor_tensor(sq, x, x, ALU.mult)
    drain_link(dve)
    nc.vector.tensor_reduce(var, sq, axis=X_AXIS, op=ALU.add)
    drain_link(dve)
    nc.vector.tensor_scalar(var, var, 1.0 / D, EPS, ALU.mult, ALU.add).then_inc(var_ready, 1)


def spread(v, groups):
    return v.unsqueeze(2).to_broadcast([P, groups, D])


def gated_sum_layer(nc, x, xt, adj, w, at, x1, mask, ident, half_power, diag, out_sem):
    BD = B * D
    PAIRS = B // 2
    JOUTER = 4
    ACCS = 5
    ctx = ExitStack()
    with ctx:
        def sb(name, shape, dt):
            return ctx.enter_context(nc.sbuf_tensor(name, shape, dt))

        def ps(name):
            return ctx.enter_context(nc.psum_tensor(name, [P, BANK], F32))

        def sem(name):
            return ctx.enter_context(nc.semaphore(name))

        xtp = sb("xtp", [P, PAIRS, N + 1], F32)
        w2 = sb("w2", [P, P], F32)
        hn = sb("hn", [P, NB, BD], F32)
        parts = sb("parts", [P, 3, NB, BD], BF16)
        rest = sb("rest", [P, 2, BD], F32)
        adjb = sb("adjb", [P, 2, HALF], I32)
        ones = sb("ones", [P, P], F32)
        hsum = sb("hsum", [P, BD], F32)
        ab = sb("ab", [P, 2, 2 * D], F32)
        xb = sb("xb0", [P, 2, BD], F32)
        t1 = sb("t1", [P, 2, BD], F32)
        t2 = sb("t2", [P, BD], F32)
        score = sb("score", [P, B], F32)
        st = sb("st0", [P, 3, B], F32)
        acc = [ps(f"acc{i}") for i in range(ACCS)]
        ph, pshift, psum = ps("ph"), ps("pshift"), ps("psum_h")

        adj_in = [sem(f"adj_in{i}") for i in range(2)]
        adj_used = sem("adj_used")
        xt_in = sem("xt_in")
        w_in = sem("w_in")
        cleared = sem("cleared")
        blk_in = [sem(f"blk_in{i}") for i in range(2)]
        blk_used = sem("blk_used")
        stored = [sem(f"stored{i}") for i in range(2)]
        h_ready = sem("h_ready")
        hs_ready = sem("hs_ready")
        hn_copied = sem("hn_copied")
        part1 = sem("part1")
        rest_ready = sem("rest_ready")
        parts_ready = sem("parts_ready")
        sum_ready = sem("sum_ready")
        sum_copied = sem("sum_copied")
        acc_ready = sem("acc_ready")
        acc_read = sem("acc_read")
        x1_ready = sem("x1_ready")
        var_ready = sem("var_ready0")
        pow_done = sem("pow_done0")
        id_ready = sem("id_ready")
        block = ctx.enter_context(nc.Block())

        xn = x.rearrange("b (k p) d -> p k b d", p=P)
        x1n = x1.rearrange("b (k p) d -> p k b d", p=P)

        @block.sync
        def _(sp):
            sp.wait_ge(cleared, 2)
            sp.dma_start(w2[0:D, 0:D], w).then_inc(w_in, 16)
            sp.dma_start(w2[D:P, D:P], w).then_inc(w_in, 16)
            for pair in range(PAIRS):
                sp.dma_start(xtp[:, pair, 2:], xt[pair, :, 1:]).then_inc(xt_in, 16)
            for k in range(NB):
                for half in range(2):
                    if k >= 1:
                        sp.wait_ge(adj_used, 2 * k + half - 1)
                    sp.dma_start(adjb[:, half, :], adj[k * P:(k + 1) * P, half * HALF:(half + 1) * HALF])\
                      .then_inc(adj_in[half], 16)

        @block.gpsimd
        def _(pool):
            nc.gpsimd.memset(w2[:], 0.0).then_inc(cleared, 1)
            nc.gpsimd.memset(xtp[:, :, 0:2], 0.0).then_inc(cleared, 1)
            nc.gpsimd.memset(ones[:], 1.0).then_inc(id_ready, 1)
            nc.gpsimd.memset(half_power[:], -0.5).then_inc(id_ready, 1)
            nc.gpsimd.memset(ident[:], 0.0).then_inc(id_ready, 1)
            pool.wait_ge(id_ready, 3)
            nc.gpsimd.affine_select(out=ident[:], in_=ident[:], compare_op=ALU.not_equal, fill=1.0,
                                    base=0, pattern=[[-1, P]], channel_multiplier=1).then_inc(id_ready, 1)
            for k in range(NB):
                pool.wait_ge(var_ready, k + 1)
                nc.gpsimd.tensor_tensor(st[:, 2, :], st[:, 1, :], half_power[:, 0:B],
                                        ALU.pow).then_inc(pow_done, 1)

        @block.tensor
        def _(pe):
            pe.wait_ge(w_in, 32)
            pe.wait_ge(xt_in, 16 * PAIRS)
            pe.wait_ge(id_ready, 4)
            for k in range(NB):
                if k >= 1:
                    pe.wait_ge(hn_copied, k)
                for pair in range(PAIRS):
                    last = nc.tensor.matmul(ph[:, pair * P:(pair + 1) * P],
                                            xtp[:, pair, 1 + k * P:1 + (k + 1) * P], w2[:],
                                            start=True, stop=True)
                last.then_inc(h_ready, 1)
                if k >= 1:
                    pe.wait_ge(rest_ready, k)
                for pair in range(PAIRS):
                    last = nc.tensor.matmul(pshift[:, pair * P:(pair + 1) * P],
                                            xtp[:, pair, k * P:(k + 1) * P], w2[:],
                                            start=True, stop=True)
                last.then_inc(hs_ready, 1)
                pe.wait_ge(hn_copied, k + 1)
                last = nc.tensor.matmul(psum[:], ones[:], hn[:, k, :], start=(k == 0), stop=(k == NB - 1))
            last.then_inc(sum_ready, 1)
            for j in range(NB):
                pe.wait_ge(adj_used, 2 * j + 2)
                pe.wait_ge(parts_ready, j + 1)
                for i in range(JOUTER):
                    for part in range(3):
                        last = nc.tensor.matmul(acc[i][:], mask[:, j, i * P:(i + 1) * P],
                                                parts[:, part, j, :], start=(j == 0 and part == 0),
                                                stop=(j == NB - 1 and part == 2))
                    if j == NB - 1:
                        last.then_inc(acc_ready, 1)
            for i in range(JOUTER, NB):
                if i >= ACCS:
                    pe.wait_ge(acc_read, i - ACCS + 1)
                for j in range(NB):
                    for part in range(3):
                        last = nc.tensor.matmul(acc[i % ACCS][:], mask[:, j, i * P:(i + 1) * P],
                                                parts[:, part, j, :], start=(j == 0 and part == 0),
                                                stop=(j == NB - 1 and part == 2))
                last.then_inc(acc_ready, 1)

        @block.scalar
        def _(act):
            for k in range(2):
                act.dma_start(xb[:, k, :].rearrange("p (b d) -> p b d", b=B), xn[:, k]).then_inc(blk_in[k], 16)
                act.dma_start(ab[:, k, :], at[k * P:(k + 1) * P, :]).then_inc(blk_in[k], 16)
            for k in range(NB):
                act.wait_ge(h_ready, k + 1)
                nc.scalar.copy(hn[:, k, :], ph[:]).then_inc(hn_copied, 1)
                act.wait_ge(hs_ready, k + 1)
                nc.scalar.copy(parts[:, 0, k, :], pshift[:]).then_inc(part1, 1)
            act.wait_ge(sum_ready, 1)
            nc.scalar.copy(hsum[:], psum[:]).then_inc(sum_copied, 1)
            for k in range(NB):
                act.wait_ge(x1_ready, k + 1)
                act.dma_start(x1n[:, k, 0:B], t1[:, k % 2, :].rearrange("p (b d) -> p b d", b=B))\
                   .then_inc(stored[k % 2], 16)
                act.dma_start(x1n[:, k, B], t1[:, k % 2, 0:D]).then_inc(stored[k % 2], 16)
                if k + 2 < NB:
                    act.wait_ge(blk_used, k + 1)
                    act.dma_start(xb[:, k % 2, :].rearrange("p (b d) -> p b d", b=B), xn[:, k + 2])\
                       .then_inc(blk_in[k % 2], 16)
                    act.dma_start(ab[:, k % 2, :], at[(k + 2) * P:(k + 3) * P, :]).then_inc(blk_in[k % 2], 16)
            for s in stored:
                act.wait_ge(s, 32 * NB // 2)

        @block.vector
        def _(dve):
            for k in range(NB):
                for half in range(2):
                    dve.wait_ge(adj_in[half], 16 * (k + 1))
                    nc.vector.tensor_scalar(mask[:, k, half * HALF:(half + 1) * HALF], adjb[:, half, :], 0,
                                            None, ALU.is_gt).then_inc(adj_used, 1)
                dve.wait_ge(part1, k + 1)
                r = rest[:, k % 2, :]
                nc.vector.tensor_tensor(r, pshift[:], parts[:, 0, k, :], ALU.subtract).then_inc(rest_ready, 1)
                drain_link(dve)
                nc.vector.tensor_copy(parts[:, 1, k, :], r)
                drain_link(dve)
                nc.vector.tensor_tensor(parts[:, 2, k, :], r, parts[:, 1, k, :], ALU.subtract)\
                  .then_inc(parts_ready, 1)
            dve.wait_ge(sum_copied, 1)
            for i in range(NB):
                t = t1[:, i % 2, :]
                t3 = t.rearrange("p (b d) -> p b d", b=B)
                dve.wait_ge(blk_in[i % 2], 32 * (i // 2 + 1))
                if i >= 2:
                    dve.wait_ge(stored[i % 2], 32 * (i // 2))
                a1 = ab[:, i % 2, 0:D].unsqueeze(1).to_broadcast([P, B, D])
                a2 = ab[:, i % 2, D:2 * D].unsqueeze(1).to_broadcast([P, B, D])
                drain_link(dve)
                nc.vector.tensor_tensor(t3, hn[:, i, :].rearrange("p (b d) -> p b d", b=B), a1, ALU.mult)
                dve.wait_ge(acc_ready, i + 1)
                nc.vector.tensor_tensor(t2[:].rearrange("p (b d) -> p b d", b=B),
                                        acc[i % ACCS][:].rearrange("p (b d) -> p b d", b=B), a2,
                                        ALU.mult).then_inc(acc_read, 1)
                drain_link(dve)
                nc.vector.tensor_tensor(t, t, t2[:], ALU.add)
                drain_link(dve)
                nc.vector.tensor_reduce(score[:], t3, axis=X_AXIS, op=ALU.add)
                drain_link(dve)
                if i == 0:
                    nc.vector.memset(score[0:1, :], 0.0)
                    drain_link(dve)
                nc.vector.tensor_tensor(t3, hsum[:].rearrange("p (b d) -> p b d", b=B),
                                        score[:].unsqueeze(2).to_broadcast([P, B, D]), ALU.mult)
                drain_link(dve)
                nc.vector.scalar_tensor_tensor(out=t, in0=t, scalar=0.2, in1=t, op0=ALU.mult, op1=ALU.max)
                drain_link(dve)
                nc.vector.tensor_tensor(t, t, xb[:, i % 2, :], ALU.add).then_inc(blk_used, 1)
                norm_start(nc, dve, t3, t2[:].rearrange("p (b d) -> p b d", b=B), st[:, 0, :], st[:, 1, :],
                           B, var_ready)
                dve.wait_ge(pow_done, i + 1)
                nc.vector.tensor_tensor(t3, t3, spread(st[:, 2, :], B), ALU.mult).then_inc(x1_ready, 1)
            for k in range(NB):
                nc.vector.tensor_scalar(mask[:, k, :], mask[:, k, :], -1.0, -MASKED, ALU.add, ALU.mult)
            drain_link(dve)
            dblocks = diagonal_blocks(mask)
            nc.vector.tensor_tensor(diag[:], dblocks, ident[:].unsqueeze(1).to_broadcast([P, NB, P]), ALU.mult)
            drain_link(dve)
            nc.vector.tensor_tensor(dblocks, dblocks, diag[:], ALU.subtract)


def diagonal_blocks(mask):
    return bass.AP(mask[:].tensor, 0, [[NB * N, P], [N + P, NB], [1, P]])


def attention_layers(nc, x1, out, whd, bh, wod, bo, gamma, beta, w2, a2, w3, a3,
                     mask, ident, half_power, diag):
    ctx = ExitStack()
    with ctx:
        def sb(name, shape, dt):
            return ctx.enter_context(nc.sbuf_tensor(name, shape, dt))

        def sem(name):
            return ctx.enter_context(nc.semaphore(name))

        xin = sb("xin", [P, NB, D], F32)
        xb = sb("xb", [P, NB, D], F32)
        wide = sb("wide", [P, 2, N], F32)
        xt = wide[0:D, 0, :]
        tmp = wide[:, 1, 0:NB * D].rearrange("p (k d) -> p k d", d=D)
        y = wide[:, 1, NB * D:2 * NB * D].rearrange("p (k d) -> p k d", d=D)
        z = sb("z", [P, NB, H * D], F32)
        zf = z[:].rearrange("p k n -> p (k n)")
        rr = zf[:, 0:N]
        sr = zf[:, N:2 * N]
        ha = [sb(f"ha{i}", [P, N], F32R) for i in range(2)]
        hb = [sb(f"hb{i}", [P, N], F32R) for i in range(2)]
        hn = [sb(f"hn{i}", [P, NB, D], F32) for i in range(3)]
        rows = sb("rows", [P, RING + 1, N], F32)
        lift = rows[:, RING, :]
        pt = sb("pt", [P, 2, N], F32)
        nm = sb("nm", [P, NB, 2], F32)
        rs = sb("rs", [P, NB], F32)
        rc = sb("rc", [P, NB], F32)
        whf = sb("whf", [P, H * 2 * D], F32)
        wh = whf[0:D, :].rearrange("p (h n) -> p h n", h=H)
        hf = whf[D:P, :]
        wo = sb("wo", [P, 2, 2 * D], F32)
        wl = sb("wl", [D, 2, D + 2], F32)
        bhs = sb("bhs", [P, H, D], F32)
        bos = sb("bos", [P, D], F32)
        gam = sb("gam", [P, D], F32)
        bet = sb("bet", [P, D], F32)
        st = sb("st", [P, 3, NB], F32)
        ls = sb("ls", [P, 2, NB], F32)
        rt = sb("rt", [P, NB], F32)
        av = tmp[0:D, 0:4, :]
        wa = tmp[0:D, 4:5, :]

        pss = ctx.enter_context(nc.psum_tensor("pss", [P, N], F32))
        tp = [ctx.enter_context(nc.psum_tensor(f"tp{i}", [P, BANK], F32)) for i in range(2)]
        po = ctx.enter_context(nc.psum_tensor("po", [P, BANK], F32))
        px = ctx.enter_context(nc.psum_tensor("px", [P, BANK], F32))

        gates = sem("gates")
        const_in = sem("const_in")
        slopes_set = sem("slopes_set")
        x_in = sem("x_in")
        resid_done = sem("resid_done")
        x_done = sem("x_done")
        x_out = sem("x_out")
        xb_free = sem("xb_free")
        x_ready = sem("x_ready")
        xt_psum = sem("xt_psum")
        xt_ready = sem("xt_ready")
        z_ready = sem("z_ready")
        zt_psum = sem("zt_psum")
        zt_ready = sem("zt_ready")
        proj_psum = sem("proj_psum")
        h1_ready = sem("h1_ready")
        h2_ready = sem("h2_ready")
        hn_psum = sem("hn_psum")
        hn_ready = sem("hn_ready")
        lr_ready = sem("lr_ready")
        right_psum = sem("right_psum")
        sr_ready = sem("sr_ready")
        rr_ready = sem("rr_ready")
        diag_set = sem("diag_set")
        scores_ready = sem("scores_ready")
        scores_read = sem("scores_read")
        mr_ready = sem("mr_ready")
        max_ready = sem("max_ready")
        exp_ready = sem("exp_ready")
        tr_ready = sem("tr_ready")
        pt_ready = sem("pt_ready")
        pv_ready = sem("pv_ready")
        out_read = sem("out_read")
        var_ready = sem("var_ready")
        pow_done = sem("pow_done")
        block = ctx.enter_context(nc.Block())

        CONSTS = 10
        HNBUF = (0, 1, 0, 1, 0, 1, 2)
        ALL_BLOCKS = UNITS * NB
        GATS, ADDS = 5, 2
        NORMS = 4

        @block.sync
        def _(sp):
            for tile, src in (
                (wh, whd.rearrange("h c n -> c h n")),
                (wo[:], wod.rearrange("(k p) n -> p k n", p=P)),
                (wl[:, 0, 0:D], w2),
                (wl[:, 1, 0:D], w3),
                (av[:, 0:2, :], a2.rearrange("(o s d) -> o s d", o=1, s=2).to_broadcast([D, 2, D])),
                (av[:, 2:4, :], a3.rearrange("(o s d) -> o s d", o=1, s=2).to_broadcast([D, 2, D])),
                (bhs[:], bh.rearrange("(o h) d -> o h d", o=1).to_broadcast([P, H, D])),
                (bos[:], bo.rearrange("(o d) -> o d", o=1).to_broadcast([P, D])),
                (gam[:], gamma.rearrange("(o d) -> o d", o=1).to_broadcast([P, D])),
                (bet[:], beta.rearrange("(o d) -> o d", o=1).to_broadcast([P, D])),
            ):
                sp.dma_start(tile, src).then_inc(const_in, 16)
            sp.dma_start(xin[:], x1[0].rearrange("(k p) d -> p k d", p=P)).then_inc(x_in, 16)
            sp.sem_inc(xb_free, 1)
            with sp.Fori(0, B) as b:
                stand_alone_wait(sp, resid_done, b * NC + NC, gates)
                sp.dma_start(xin[:], x1[bass.ds(b + 1, 1)].rearrange("o (k p) d -> p (o k) d", p=P))\
                  .then_inc(x_in, 16)
                dst = out[bass.ds(b, 1)].rearrange("o (k p) d -> p (o k) d", p=P)
                for c in range(NC):
                    blocks = slice(c * CH, (c + 1) * CH)
                    stand_alone_wait(sp, x_done, b * NC + c + 1, gates)
                    sp.dma_start(dst[:, blocks, :], xb[:, blocks, :]).then_inc(x_out, 16)
                stand_alone_wait(sp, x_out, b * (16 * NC) + 16 * NC, gates)
                sp.sem_inc(xb_free, 1)
            sp.wait_ge(x_out, B * 16 * NC)

        @block.gpsimd
        def _(pool):
            norms = Count(var_ready, NORMS * NC)
            sr_c = Count(sr_ready, ADDS * NC)
            tr_c = Count(tr_ready, ALL_BLOCKS * NC)
            counts = (norms, sr_c, tr_c)

            def run_side(units, step):
                for _, name, c in tasks_at(units, step):
                    if name in ("lna", "lnb", "ra"):
                        norms.n += 1
                        cols = slice(c * CH, (c + 1) * CH)
                        stand_alone_wait(pool, norms.sem, norms.value(), gates)
                        nc.gpsimd.tensor_tensor(st[:, 2, cols], st[:, 1, cols], half_power[:, 0:CH], ALU.pow)\
                          .then_inc(pow_done, 1)

            pool.sem_inc(diag_set, 1)
            with pool.Fori(0, B) as b:
                enter_loop(counts, b)
                for units in GROUPS:
                    blocks = len(units) * NB
                    additive = units[0] >= ADD1
                    if additive:
                        sr_c.n += NC
                        stand_alone_wait(pool, sr_c.sem, sr_c.value(), gates)
                    if units[0] == ADD2:
                        nc.gpsimd.tensor_tensor(diagonal_blocks(mask), diagonal_blocks(mask), diag[:],
                                                ALU.add).then_inc(diag_set, 1)
                        stand_alone_wait(pool, diag_set, b * 2 + 2, gates)
                    for g in range(blocks + 2):
                        if additive and g < NB:
                            if g >= RING:
                                stand_alone_wait(pool, tr_c.sem, tr_c.value(tr_c.n + 4 * (g - RING + 1)), gates)
                            nc.gpsimd.tensor_tensor(rows[:, g % RING, :], sr, mask[:, g, :], ALU.add)\
                              .then_inc(mr_ready, 1)
                        run_side(units, g)
                    run_side(units, None)
                    if units[0] == ADD2:
                        stand_alone_wait(pool, mr_ready, b * (ADDS * NB) + ADDS * NB, gates)
                        nc.gpsimd.tensor_tensor(diagonal_blocks(mask), diagonal_blocks(mask), diag[:],
                                                ALU.subtract).then_inc(diag_set, 1)
                    tr_c.n += 4 * blocks
                leave_loop(counts)

        @block.tensor
        def _(pe):
            x_c = Count(x_in, 16)
            xr_c = Count(x_ready, ADDS * NC)
            xt_c = Count(xt_ready, 3 * NC)
            z_c = Count(z_ready, H * NC)
            zt_c = Count(zt_ready, 2 * NC)
            h1_c = Count(h1_ready, GATS * NC)
            h2_c = Count(h2_ready, GATS * NC)
            hn_c = Count(hn_ready, UNITS * NC)
            lr_c = Count(lr_ready, ADDS * NC)
            rr_c = Count(rr_ready, ADDS * NC)
            read_c = Count(scores_read, GATS * 2 * NB)
            exp_c = Count(exp_ready, ALL_BLOCKS)
            pt_c = Count(pt_ready, ALL_BLOCKS * NC)
            out_c = Count(out_read, ALL_BLOCKS)
            counts = (x_c, xr_c, xt_c, z_c, zt_c, h1_c, h2_c, hn_c, lr_c, rr_c, read_c, exp_c, pt_c, out_c)
            tiles = [0]
            px_reader = [None]

            def wait(count, n=None):
                stand_alone_wait(pe, count.sem, count.value(n), gates)

            def px_free():
                if px_reader[0] is not None:
                    wait(px_reader[0])

            def px_used(count):
                count.n += 1
                px_reader[0] = count

            def run_task(unit, name, c):
                cols = slice(c * BANK, (c + 1) * BANK)
                if name in ("xt", "xn"):
                    px_free()
                    if name == "xn" and c == 0:
                        x_c.n += 16
                        wait(x_c)
                    if name == "xt":
                        xr_c.n += 1
                        wait(xr_c)
                    src = xin if name == "xn" else xb
                    for q in range(CH):
                        last = nc.tensor.transpose(px[0:D, q * P:(q + 1) * P], src[:, c * CH + q, :], ident[:])
                    last.then_inc(xt_psum, 1)
                    px_used(xt_c)
                elif name in ("z0", "z1"):
                    k = int(name[1])
                    px_free()
                    if k == 0:
                        z_c.n += 1 if c else (H - 1) * NC + 1
                        wait(z_c)
                    for q in range(CH):
                        last = nc.tensor.transpose(px[:, q * P:(q + 1) * P],
                                                   z[:, c * CH + q, k * P:(k + 1) * P], ident[:])
                    last.then_inc(zt_psum, 1)
                    px_used(zt_c)
                elif name == "proj":
                    to = next_gat(unit)
                    px_free()
                    if to == GAT2:
                        for k in range(2):
                            last = nc.tensor.matmul(px[:], wo[:, k, :], wide[:, k, cols],
                                                    start=(k == 0), stop=(k == 1))
                    else:
                        last = nc.tensor.matmul(px[:], wh[:, to, :], xt[:, cols], start=True, stop=True)
                    last.then_inc(proj_psum, 1)
                    px_used(h2_c)
                    h1_c.n += 1
                elif name == "hn":
                    px_free()
                    for q in range(CH):
                        last = nc.tensor.transpose(px[:, q * D:(q + 1) * D], hf[:, q * P:(q + 1) * P],
                                                   ident[D:P, D:P])
                    last.then_inc(hn_psum, 1)
                    px_used(hn_c)
                elif name == "h":
                    px_free()
                    for q in range(CH):
                        k = c * CH + q
                        last = nc.tensor.matmul(px[:, q * (D + 2):(q + 1) * (D + 2)], xt[:, k * P:(k + 1) * P],
                                                wl[:, unit - GAT2, :], start=True, stop=True)
                    last.then_inc(hn_psum, 1)
                    px_used(lr_c)
                    hn_c.n += 1
                elif name == "r":
                    px_free()
                    wait(lr_c)
                    for q in range(CH):
                        k = c * CH + q
                        last = nc.tensor.transpose(px[:, q * P:(q + 1) * P],
                                                   rt[:, k:k + 1].to_broadcast([P, P]), ident[:])
                    last.then_inc(right_psum, 1)
                    px_used(rr_c)

            def run_side(units, step):
                for unit, name, c in tasks_at(units, step):
                    run_task(unit, name, c)

            def run_group(units):
                blocks = len(units) * NB
                gat = units[0] <= GAT2
                exp0, pt0, out0, read0 = exp_c.n, pt_c.n, out_c.n, read_c.n
                for g in range(blocks + 2):
                    if g < blocks and g % NB == 0:
                        if gat:
                            wait(h2_c)
                        wait(hn_c)
                    if gat and g < blocks:
                        unit, t = units[g // NB], g % NB
                        rows_t = slice(t * P, (t + 1) * P)
                        for half in range(2):
                            if g >= 1:
                                wait(read_c, read0 + 2 * (g - 1) + half + 1)
                            for c in range(half * NC // 2, (half + 1) * NC // 2):
                                cols = slice(c * BANK, (c + 1) * BANK)
                                moving = ha[unit % 2][:, cols]
                                nc.tensor.matmul(pss[:, cols], ha[unit % 2][:, rows_t], moving,
                                                 start=True, stop=False)
                                last = nc.tensor.matmul(pss[:, cols], hb[unit % 2][:, rows_t], moving,
                                                        start=False, stop=True)
                            last.then_inc(scores_ready, 1)
                    run_side(units, g)
                    for q in range(4):
                        if 1 <= g <= blocks:
                            if q == 0:
                                wait(exp_c, exp0 + g)
                            if tiles[0] >= 2:
                                wait(pt_c, pt0 + 4 * (g - 1) + q - 1)
                            bank = tp[tiles[0] % 2]
                            tiles[0] += 1
                            for s in range(4):
                                jb = 4 * q + s
                                last = nc.tensor.transpose(bank[:, s * P:(s + 1) * P],
                                                           rows[:, (g - 1) % RING, jb * P:(jb + 1) * P],
                                                           ident[:])
                            last.then_inc(tr_ready, 1)
                        if g >= 2:
                            nodes = hn[HNBUF[units[(g - 2) // NB]]]
                            if q == 0:
                                wait(pt_c, pt0 + 4 * (g - 1))
                                if g >= 3:
                                    wait(out_c, out0 + g - 2)
                            for jb in range(4 * q, 4 * q + 4):
                                last = nc.tensor.matmul(po[:, 0:D], pt[:, g % 2, jb * P:(jb + 1) * P],
                                                        nodes[:, jb, :], start=(jb == 0),
                                                        stop=(jb == NB - 1))
                            if q == 3:
                                last.then_inc(pv_ready, 1)
                exp_c.n += blocks
                pt_c.n += 4 * blocks
                out_c.n += blocks
                if gat:
                    read_c.n += 2 * blocks
                run_side(units, None)

            pe.wait_ge(const_in, 16 * CONSTS)
            pe.wait_ge(slopes_set, 1)
            for c in range(NC):
                run_task(ADD2, "xn", c)
            for c in range(NC):
                run_task(ADD2, "proj", c)
                run_task(ADD2, "hn", c)
            with pe.Fori(0, B) as b:
                enter_loop(counts, b)
                tiles[0] = 0
                for units in GROUPS:
                    run_group(units)
                leave_loop(counts)

        @block.scalar
        def _(act):
            xt_c = Count(xt_psum, 3 * NC)
            zt_c = Count(zt_psum, 2 * NC)
            proj_c = Count(proj_psum, GATS * NC)
            hn_c = Count(hn_psum, UNITS * NC)
            right_c = Count(right_psum, ADDS * NC)
            max_c = Count(max_ready, ADDS * NB)
            read_c = Count(scores_read, GATS * 2 * NB)
            tr_c = Count(tr_ready, ALL_BLOCKS * NC)
            pv_c = Count(pv_ready, ALL_BLOCKS)
            counts = (xt_c, zt_c, proj_c, hn_c, right_c, max_c, read_c, tr_c, pv_c)
            tiles = [0]

            def wait(count, n=None):
                stand_alone_wait(act, count.sem, count.value(n), gates)

            def next_of(count):
                count.n += 1
                wait(count)

            def run_task(unit, name, c):
                cols = slice(c * BANK, (c + 1) * BANK)
                blocks = slice(c * CH, (c + 1) * CH)
                if name in ("xt", "xn"):
                    next_of(xt_c)
                    nc.scalar.copy(xt[:, cols], px[0:D, :]).then_inc(xt_ready, 1)
                elif name in ("z0", "z1"):
                    next_of(zt_c)
                    nc.scalar.copy(wide[:, int(name[1]), cols], px[:]).then_inc(zt_ready, 1)
                elif name == "proj":
                    i = next_gat(unit) % 2
                    next_of(proj_c)
                    nc.scalar.copy(ha[i][0:D, cols], px[0:D, :])
                    nc.scalar.copy(hb[i][D:P, cols], px[D:P, :])
                    nc.scalar.copy(hf, px[D:P, :]).then_inc(h1_ready, 1)
                elif name == "hn":
                    next_of(hn_c)
                    nc.scalar.copy(hn[HNBUF[next_gat(unit)]][:, blocks, :],
                                   px[:, 0:CH * D].rearrange("p (k d) -> p k d", d=D)).then_inc(hn_ready, 1)
                elif name == "h":
                    next_of(hn_c)
                    nc.scalar.copy(hn[HNBUF[unit + 1]][:, blocks, :],
                                   px[:, 0:CH * (D + 2)].rearrange("p (k d) -> p k d", d=D + 2)[:, :, 0:D])\
                      .then_inc(hn_ready, 1)
                elif name == "r":
                    next_of(right_c)
                    nc.scalar.mul(sr[:, cols], px[:], SLOPES[unit + 1]).then_inc(sr_ready, 1)

            def run_side(units, step):
                for unit, name, c in tasks_at(units, step):
                    run_task(unit, name, c)

            def run_group(units):
                blocks = len(units) * NB
                max0, read0, tr0, pv0 = max_c.n, read_c.n, tr_c.n, pv_c.n

                def copy_tile(g, q):
                    if q == 0 and g >= 2:
                        wait(pv_c, pv0 + g - 1)
                    wait(tr_c, tr0 + 4 * g + q + 1)
                    nc.scalar.copy(pt[:, g % 2, q * BANK:(q + 1) * BANK], tp[tiles[0] % 2][:])\
                      .then_inc(pt_ready, 1)
                    tiles[0] += 1

                for g in range(blocks + 2):
                    if 1 <= g <= blocks:
                        copy_tile(g - 1, 0)
                        copy_tile(g - 1, 1)
                    if g < blocks:
                        t = g % NB
                        if units[0] <= GAT2:
                            wait(read_c, read0 + 2 * g + 2)
                        else:
                            wait(max_c, max0 + g + 1)
                        nc.scalar.activation(rows[:, g % RING, :], rows[:, g % RING, :], ACT.Exp, scale=-1.0,
                                             bias=nm[:, t, 1:2], accum_out=rs[:, t:t + 1])\
                          .then_inc(exp_ready, 1)
                    run_side(units, g)
                    if 1 <= g <= blocks:
                        copy_tile(g - 1, 2)
                        copy_tile(g - 1, 3)
                if units[0] <= GAT2:
                    read_c.n += 2 * blocks
                else:
                    max_c.n += blocks
                tr_c.n += 4 * blocks
                pv_c.n += blocks
                run_side(units, None)

            for c in range(NC):
                run_task(ADD2, "xn", c)
            for c in range(NC):
                run_task(ADD2, "proj", c)
                run_task(ADD2, "hn", c)
            with act.Fori(0, B) as b:
                enter_loop(counts, b)
                tiles[0] = 0
                for units in GROUPS:
                    run_group(units)
                leave_loop(counts)

        @block.vector
        def _(dve):
            h1_c = Count(h1_ready, GATS * NC)
            hn_c = Count(hn_ready, UNITS * NC)
            sr_c = Count(sr_ready, ADDS * NC)
            x_c = Count(x_in, 16)
            free_c = Count(xb_free, 1)
            pow_c = Count(pow_done, NORMS * NC)
            scores_c = Count(scores_ready, GATS * 2 * NB)
            mr_c = Count(mr_ready, ADDS * NB)
            tr_c = Count(tr_ready, ALL_BLOCKS * NC)
            pv_c = Count(pv_ready, ALL_BLOCKS)
            counts = (h1_c, hn_c, sr_c, x_c, free_c, pow_c, scores_c, mr_c, tr_c, pv_c)

            def wait(count, n=None):
                stand_alone_wait(dve, count.sem, count.value(n), gates)

            def next_of(count):
                count.n += 1
                wait(count)

            def each(v):
                return v[:].unsqueeze(1).to_broadcast([P, CH, D])

            def run_task(unit, name, c):
                cols = slice(c * BANK, (c + 1) * BANK)
                blocks = slice(c * CH, (c + 1) * CH)
                yc, xc, sq = y[:, blocks, :], xb[:, blocks, :], tmp[:, blocks, :]
                sums, var, rstd = (st[:, n, blocks] for n in range(3))
                if name == "proj":
                    i = next_gat(unit) % 2
                    next_of(h1_c)
                    nc.vector.tensor_tensor(ha[i][D:P, cols], px[D:P, :], hb[i][D:P, cols].bitcast(F32),
                                            ALU.subtract)
                    nc.vector.tensor_tensor(hb[i][0:D, cols], px[0:D, :], ha[i][0:D, cols].bitcast(F32),
                                            ALU.subtract).then_inc(h2_ready, 1)
                elif name == "hn":
                    hn_c.n += 1
                elif name == "h":
                    next_of(hn_c)
                    pair = px[:, 0:CH * (D + 2)].rearrange("p (k d) -> p k d", d=D + 2)
                    nc.vector.tensor_scalar(ls[:, (unit + 1) % 2, blocks].unsqueeze(2), pair[:, :, D:D + 1],
                                            1.0 - SLOPES[unit + 1], None, ALU.mult)
                    nc.vector.tensor_copy(rt[:, blocks].unsqueeze(2), pair[:, :, D + 1:D + 2])\
                      .then_inc(lr_ready, 1)
                elif name == "r":
                    next_of(sr_c)
                    nc.vector.tensor_scalar(rr[:, cols], px[:], 1.0 - SLOPES[unit + 1], None, ALU.mult)\
                      .then_inc(rr_ready, 1)
                elif name == "lna":
                    drain_link(dve)
                    nc.vector.scalar_tensor_tensor(out=yc, in0=yc, scalar=0.2, in1=yc, op0=ALU.mult,
                                                   op1=ALU.max)
                    norm_start(nc, dve, yc, sq, sums, var, CH, var_ready)
                elif name == "lnb":
                    next_of(pow_c)
                    nc.vector.tensor_tensor(yc, yc, spread(rstd, CH), ALU.mult)
                    drain_link(dve)
                    nc.vector.tensor_tensor(yc, yc, each(gam), ALU.mult)
                    drain_link(dve)
                    nc.vector.tensor_tensor(yc, yc, each(bet), ALU.add)
                    if c == 0:
                        x_c.n += 16
                        wait(x_c)
                        next_of(free_c)
                    drain_link(dve)
                    nc.vector.tensor_tensor(xc, xin[:, blocks, :], yc, ALU.add).then_inc(resid_done, 1)
                    norm_start(nc, dve, xc, sq, sums, var, CH, var_ready)
                elif name in ("lnc", "rb"):
                    next_of(pow_c)
                    drain_link(dve)
                    nc.vector.tensor_tensor(xc, xc, spread(rstd, CH), ALU.mult)\
                      .then_inc(x_done if unit == ADD2 else x_ready, 1)
                elif name == "ra":
                    drain_link(dve)
                    nc.vector.tensor_tensor(xc, xc, yc, ALU.add)
                    norm_start(nc, dve, xc, sq, sums, var, CH, var_ready)

            def run_side(units, step):
                for unit, name, c in tasks_at(units, step):
                    run_task(unit, name, c)

            def run_group(units):
                blocks = len(units) * NB
                gat = units[0] <= GAT2
                tr0, pv0, sc0, mr0 = tr_c.n, pv_c.n, scores_c.n, mr_c.n
                if units[0] == 0:
                    stand_alone_wait(dve, diag_set, diag_c.value(1), gates)

                def lift_block(t):
                    nc.vector.tensor_scalar(lift, rr, ls[:, units[0] % 2, t:t + 1], 0.0, ALU.add, ALU.max)

                if not gat:
                    lift_block(0)
                for g in range(blocks + 2):
                    if g < blocks:
                        t = g % NB
                        scores = rows[:, g % RING, :]
                        if gat:
                            if g >= RING:
                                wait(tr_c, tr0 + 4 * (g - RING + 1))
                            for half in range(2):
                                cols = slice(half * HALF, (half + 1) * HALF)
                                wait(scores_c, sc0 + 2 * g + half + 1)
                                nc.vector.tensor_tensor_reduce(
                                    out=rows[:, g % RING, cols], in0=pss[:, cols], in1=mask[:, t, cols],
                                    scale=-1.0, scalar=(-2 * MASKED if half == 0 else nm[:, t, 0:1]),
                                    op0=ALU.add, op1=ALU.min,
                                    accum_out=nm[:, t, half:half + 1]).then_inc(scores_read, 1)
                                if half == 0:
                                    drain_link(dve)
                        else:
                            wait(mr_c, mr0 + g + 1)
                            drain_link(dve)
                            nc.vector.tensor_tensor_reduce(
                                out=scores, in0=lift, in1=scores, scale=-1.0, scalar=-2 * MASKED,
                                op0=ALU.add, op1=ALU.min, accum_out=nm[:, t, 1:2]).then_inc(max_ready, 1)
                    run_side(units, g)
                    if not gat and g + 1 < blocks:
                        drain_link(dve)
                        lift_block(g + 1)
                    if g >= 2:
                        unit, u = units[(g - 2) // NB], (g - 2) % NB
                        wait(pv_c, pv0 + g - 1)
                        nc.vector.reciprocal(rc[:, u:u + 1], rs[:, u:u + 1])
                        drain_link(dve)
                        if gat:
                            bias = bhs[:, unit, :] if unit < H else bos[:]
                            nc.vector.scalar_tensor_tensor(out=y[:, u, :], in0=po[:, 0:D],
                                                           scalar=rc[:, u:u + 1], in1=bias, op0=ALU.mult,
                                                           op1=ALU.add).then_inc(out_read, 1)
                        else:
                            nc.vector.tensor_scalar(y[:, u, :], po[:, 0:D], rc[:, u:u + 1], None, ALU.mult)\
                              .then_inc(out_read, 1)
                        if unit < H and u % CH == CH - 1:
                            blk = slice(u + 1 - CH, u + 1)
                            drain_link(dve)
                            nc.vector.scalar_tensor_tensor(out=z[:, blk, unit * D:(unit + 1) * D],
                                                           in0=y[:, blk, :], scalar=0.2,
                                                           in1=y[:, blk, :], op0=ALU.mult,
                                                           op1=ALU.max).then_inc(z_ready, 1)
                            drain_link(dve)
                tr_c.n += 4 * blocks
                pv_c.n += blocks
                if gat:
                    scores_c.n += 2 * blocks
                else:
                    mr_c.n += blocks
                run_side(units, None)
                drain_link(dve)

            diag_c = Count(diag_set, 2)
            dve.wait_ge(const_in, 16 * CONSTS)
            for k in range(2):
                for side in range(2):
                    drain_link(dve)
                    nc.vector.tensor_tensor(wa, wl[:, k:k + 1, 0:D], av[:, 2 * k + side:2 * k + side + 1, :],
                                            ALU.mult)
                    drain_link(dve)
                    last = nc.vector.tensor_reduce(wl[:, k, D + side:D + side + 1], wa, axis=X_AXIS, op=ALU.add)
            last.then_inc(slopes_set, 1)
            for c in range(NC):
                run_task(ADD2, "proj", c)
                run_task(ADD2, "hn", c)
            with dve.Fori(0, B) as b:
                enter_loop(counts, b)
                diag_c.batch = b
                for units in GROUPS:
                    run_group(units)
                leave_loop(counts)


def build(nc, x, xt, adj, w0, a0, whd, bh, wod, bo, gamma, beta, w2, a2, w3, a3, out):
    x1 = nc.dram_tensor("x1", [B + 1, N, D], F32).ap()
    with ExitStack() as ctx:
        mask = ctx.enter_context(nc.sbuf_tensor("mask", [P, NB, N], BF16))
        diag = ctx.enter_context(nc.sbuf_tensor("diag", [P, NB, P], BF16))
        ident = ctx.enter_context(nc.sbuf_tensor("ident", [P, P], F32))
        half_power = ctx.enter_context(nc.sbuf_tensor("half_power", [P, NB], F32))
        gated_sum_layer(nc, x, xt, adj, w0, a0, x1, mask, ident, half_power, diag, None)
        attention_layers(nc, x1, out, whd, bh, wod, bo, gamma, beta, w2, a2, w3, a3,
                         mask, ident, half_power, diag)


def kernel(x, adj, L0_gnn_W, L0_gnn_a, L1_gnn_Wh, L1_gnn_bh, L1_gnn_Wo, L1_gnn_bo, L1_gnn_gamma,
           L1_gnn_beta, L2_gnn_weight, L2_gnn_a, L3_gnn_W, L3_gnn_a):
    import numpy as np
    import concourse.bacc as bacc
    from concourse.bass_utils import run_bass_kernel_spmd as run

    def c(v):
        return np.ascontiguousarray(v)

    x = np.asarray(x)
    wh = np.asarray(L1_gnn_Wh).transpose(0, 2, 1)
    wo = np.asarray(L1_gnn_Wo).T
    arrays = {
        "x": c(x),
        "xt": c(x.transpose(0, 2, 1).reshape(B // 2, 2 * D, N)),
        "adj": c(adj),
        "w0": c(L0_gnn_W),
        "a0": c(np.asarray(L0_gnn_a).T),
        "whd": c(np.concatenate([wh, wh], axis=2)),
        "bh": c(L1_gnn_bh),
        "wod": c(np.concatenate([wo, wo], axis=1)),
        "bo": c(L1_gnn_bo),
        "gamma": c(L1_gnn_gamma),
        "beta": c(L1_gnn_beta),
        "w2": c(L2_gnn_weight),
        "a2": c(np.asarray(L2_gnn_a).reshape(-1)),
        "w3": c(L3_gnn_W),
        "a3": c(L3_gnn_a),
    }
    nc = bacc.Bacc("TRN2", target_bir_lowering=False, num_devices=1)
    args = [nc.dram_tensor(f"in_{n}", a.shape, mybir.dt.from_np(a.dtype), kind="ExternalInput").ap()
            for n, a in arrays.items()]
    out = nc.dram_tensor("out_0", [B, N, D], F32, kind="ExternalOutput").ap()
    build(nc, *args, out)
    r = run(nc, [{f"in_{n}": a for n, a in arrays.items()}], core_ids=[0])
    return r.results[0]["out_0"]
```

```python
import concourse.bass as bass
from concourse import mybir
from contextlib import ExitStack

F32 = mybir.dt.float32
F32R = mybir.dt.float32r
BF16 = mybir.dt.bfloat16
I32 = mybir.dt.int32
ALU = mybir.AluOpType
ACT = mybir.ActivationFunctionType
X_AXIS = mybir.AxisListType.X

B, N, D = 8, 2048, 64
P = 128
NB = N // P
H = 4
BANK = 512
NC = N // BANK
HALF = N // 2
MASKED = -1.0e30
EMPTY = -1.0e29
EPS = 1e-5
UNITS = 7
GAT2, ADD1, ADD2 = H, H + 1, H + 2
SLOPES = {ADD1: 0.01, ADD2: 0.2}
CH = NB // NC
RING = 3
PROJ = {GAT2: 0, 0: 1, 1: 0, 2: 1, 3: 0}


class Row:

    def __init__(self, unit, t, hn, k):
        self.unit, self.t, self.hn, self.k = unit, t, hn, k
        self.gat = unit <= GAT2


class Segment:

    def __init__(self, units, gap, carried, ahead, tasks):
        self.first = 2 if carried else 0
        self.rows, self.tasks, self.starts = [], {}, []
        self.blocks = len(units) * NB
        k = n_gat = n_add = act_tiles = dve_tiles = 0
        if ahead:
            units = units + [(GAT2, 2)]
        for n, (unit, hn) in enumerate(units):
            if n and (gap == "all" or (gap == "last" and n == len(units) - 1)):
                self.rows += [None] * 3
            self.starts.append(len(self.rows))
            for t in range(NB if k < self.blocks else 2):
                row = Row(unit, t, hn, k)
                row.slot = 1 if k == self.blocks - 1 and k % RING == 0 else (k % self.blocks) % RING
                row.nth = n_gat if row.gat else n_add
                row.copier, row.count = [], []
                for q in range(NC):
                    by_dve = not row.gat and q % 2 == 1
                    row.copier.append("dve" if by_dve else "act")
                    row.count.append(dve_tiles if by_dve else act_tiles)
                    dve_tiles, act_tiles = dve_tiles + by_dve, act_tiles + (not by_dve)
                self.rows.append(row)
                n_gat, n_add, k = n_gat + row.gat, n_add + (not row.gat), k + 1
        blocks = [r for r in self.rows if r]
        for row in blocks:
            before = [r.k for r in blocks[:row.k] if r.slot == row.slot]
            row.slot_user = before[-1] if before else row.k - RING
            row.before = blocks[row.k - 1] if row.k else None
        own = [r for r in blocks if r.k < self.blocks]
        self.gats = sum(r.gat for r in own)
        self.adds = len(own) - self.gats
        self.act_tiles = sum(r.copier.count("act") for r in own)
        self.dve_tiles = sum(r.copier.count("dve") for r in own)
        self.steps = range(self.first, len(self.rows) + (0 if ahead else 2))
        for step, name, unit, c in tasks:
            self.tasks.setdefault(step, []).append((name, unit, c))
        assert all(k in ("before", "after") or k in self.steps for k in self.tasks), self.tasks.keys()

    def row(self, step):
        return self.rows[step] if 0 <= step < len(self.rows) else None

    def tally(self, *names):
        return sum(name in names for tasks in self.tasks.values() for name, _, _ in tasks)


def prologue():
    tasks = [("before", name, 0, c) for name in ("xn",) for c in range(NC)]
    tasks += [("before", name, 0, c) for c in range(NC) for name in ("proj", "hn")]
    for u in range(H - 1):
        for c in range(NC):
            tasks += [(NB * u + 2 + 3 * c, "proj", u + 1, c), (NB * u + 3 + 3 * c, "hn", u + 1, c)]
    tasks += [(NB * H + 2, name, GAT2, c) for c in range(NC) for name in ("z0", "z1", "proj", "hn")]
    return Segment([(0, 1), (1, 2), (2, 1), (3, 2)], "last", False, True, tasks)


def main_loop():
    tasks = []
    a1, h1, h2, h3, a2 = (NB * n for n in range(2, 7))
    for c in range(NC):
        n = CH * c
        tasks += [(2 + 3 * c, "xn", 0, c), (3 + 3 * c, "proj", 0, c), (4 + 3 * c, "hn", 0, c)]
        tasks += [(7 + n, "lna", GAT2, c), (10 + n, "lnb", GAT2, c), (13 + n, "lnc", GAT2, c)]
        tasks += [(15 + n, "xt", ADD1, c), (16 + n, "h", ADD1, c), (17 + n, "r", ADD1, c)]
        p1, n1 = ((a1 - 2, a1 - 1), (a1 + 1, a1 + 2), (a1 + 5, a1 + 6), (a1 + 9, a1 + 10))[c]
        tasks += [(p1, "proj", 1, c), (n1, "hn", 1, c)]
        tasks += [(h1 + 3 + 2 * c, "ra", ADD1, c), (h1 + 5 + 2 * c, "rb", ADD1, c)]
        tasks += [(h1 + 2 * c, "proj", 2, c), (h1 + 1 + 2 * c, "hn", 2, c)]
        tasks += [(h1 + 8 + 3 * c, "xt", ADD2, c), (h1 + 9 + 3 * c, "h", ADD2, c), (h1 + 10 + 3 * c, "r", ADD2, c)]
        tasks += [(h2 + 4 + 2 * c, "proj", 3, c), (h2 + 5 + 2 * c, "hn", 3, c)]
        z = (h3 + 7, h3 + 11, a2 + 5, a2 + 9)[c]
        tasks += [(z, "z0", GAT2, c), (z + 1, "z1", GAT2, c)]
        m = (a2 + 1, a2 + 3, a2 + 7, a2 + 11)[c]
        tasks += [(m, "proj", GAT2, c), (m + 1, "hn", GAT2, c)]
        tasks += [(h3 + 4 + n, "close", h3 + n + 3, c), (a2 + 3 + n, "open", a2 + n + 3, c)]
        ra, rb = (a2 + 6 + n, a2 + 8 + n) if c < NC - 1 else ("after", "after")
        tasks += [(ra, "ra", ADD2, c), (rb, "rb", ADD2, c)]
    return Segment([(GAT2, 2), (0, 1), (ADD1, 0), (1, 2), (2, 1), (3, 2), (ADD2, 0)], None, True, True, tasks)


def epilogue():
    tasks = []
    a1, a2 = NB + 3, 2 * (NB + 3)
    for c in range(NC):
        n = CH * c
        tasks += [(min(n + 6 + m, a1 - 1), name, GAT2, c) for m, name in enumerate(("lna", "lnb", "lnc"))]
        tasks += [(min(n + 9 + m, a1 - 1), name, ADD1, c) for m, name in enumerate(("xt", "h", "r"))]
        tasks += [(min(a1 + n + 6 + m, a2 - 1), name, ADD1, c) for m, name in enumerate(("ra", "rb"))]
        tasks += [(min(a1 + n + 8 + m, a2 - 1), name, ADD2, c) for m, name in enumerate(("xt", "h"))]
        tasks += [(a2 - 1, "r", ADD2, c), (a1 + n + 3, "close", NB + n + 3, c)]
        ra, rb = (a2 + 6 + n, a2 + 7 + n) if c < NC - 1 else ("after", "after")
        tasks += [(ra, "ra", ADD2, c), (rb, "rb", ADD2, c)]
    return Segment([(GAT2, 2), (ADD1, 0), (ADD2, 1)], "all", True, False, tasks)


PROLOGUE, LOOP, EPILOGUE = prologue(), main_loop(), epilogue()


class Count:

    def __init__(self, sem, each):
        self.sem, self.each, self.n, self.batch = sem, each, 0, None

    def value(self, n=None):
        n = self.n if n is None else n
        return n if self.batch is None else self.batch * self.each + n


def enter_loop(counts, b):
    for c in counts:
        c.batch, c.start = b, c.n


def leave_loop(counts):
    for c in counts:
        assert c.n - c.start == c.each, (c.sem, c.n - c.start, c.each)
        c.batch, c.n = None, c.start + (B - 1) * c.each


def run_segments(eng, counts, run):
    run(PROLOGUE)
    with eng.Fori(0, B - 1) as b:
        enter_loop(counts, b)
        run(LOOP)
        leave_loop(counts)
    run(EPILOGUE)


def drain_link(eng):
    eng.drain()


def stand_alone_wait(eng, sem, value, gates):
    eng.wait_ge(sem, value)
    eng.sem_inc(gates, 1)


def norm_start(nc, dve, x, sq, sums, var, groups, var_ready):
    drain_link(dve)
    nc.vector.tensor_reduce(sums, x, axis=X_AXIS, op=ALU.add)
    drain_link(dve)
    nc.vector.scalar_tensor_tensor(out=x, in0=spread(sums, groups), scalar=-1.0 / D, in1=x,
                                   op0=ALU.mult, op1=ALU.add)
    drain_link(dve)
    nc.vector.tensor_tensor(sq, x, x, ALU.mult)
    drain_link(dve)
    nc.vector.tensor_reduce(var, sq, axis=X_AXIS, op=ALU.add)
    drain_link(dve)
    nc.vector.tensor_scalar(var, var, 1.0 / D, EPS, ALU.mult, ALU.add).then_inc(var_ready, 1)


def spread(v, groups):
    return v.unsqueeze(2).to_broadcast([P, groups, D])


def gated_sum_layer(nc, x, xt, adj, w, at, x1, mask, ident, half_power, diag, out_sem):
    BD = B * D
    PAIRS = B // 2
    JOUTER = 4
    ACCS = 5
    ctx = ExitStack()
    with ctx:
        def sb(name, shape, dt):
            return ctx.enter_context(nc.sbuf_tensor(name, shape, dt))

        def ps(name):
            return ctx.enter_context(nc.psum_tensor(name, [P, BANK], F32))

        def sem(name):
            return ctx.enter_context(nc.semaphore(name))

        xtp = sb("xtp", [P, PAIRS, N + 1], F32)
        w2 = sb("w2", [P, P], F32)
        hn = sb("hn", [P, NB, BD], F32)
        parts = sb("parts", [P, 3, NB, BD], BF16)
        rest = sb("rest", [P, 2, BD], F32)
        adjb = sb("adjb", [P, 2, HALF], I32)
        ones = sb("ones", [P, P], F32)
        hsum = sb("hsum", [P, BD], F32)
        ab = sb("ab", [P, 2, 2 * D], F32)
        xb = sb("xb0", [P, 2, BD], F32)
        t1 = sb("t1", [P, 2, BD], F32)
        t2 = sb("t2", [P, BD], F32)
        score = sb("score", [P, B], F32)
        st = sb("st0", [P, 3, B], F32)
        acc = [ps(f"acc{i}") for i in range(ACCS)]
        ph, pshift, psum = ps("ph"), ps("pshift"), ps("psum_h")

        adj_in = [sem(f"adj_in{i}") for i in range(2)]
        adj_used = sem("adj_used")
        xt_in = sem("xt_in")
        w_in = sem("w_in")
        cleared = sem("cleared")
        blk_in = [sem(f"blk_in{i}") for i in range(2)]
        blk_used = sem("blk_used")
        stored = [sem(f"stored{i}") for i in range(2)]
        h_ready = sem("h_ready")
        hs_ready = sem("hs_ready")
        hn_copied = sem("hn_copied")
        part1 = sem("part1")
        rest_ready = sem("rest_ready")
        parts_ready = sem("parts_ready")
        sum_ready = sem("sum_ready")
        sum_copied = sem("sum_copied")
        acc_ready = sem("acc_ready")
        acc_read = sem("acc_read")
        x1_ready = sem("x1_ready")
        var_ready = sem("var_ready0")
        pow_done = sem("pow_done0")
        id_ready = sem("id_ready")
        block = ctx.enter_context(nc.Block())

        xn = x.rearrange("b (k p) d -> p k b d", p=P)
        x1n = x1.rearrange("b (k p) d -> p k b d", p=P)

        @block.sync
        def _(sp):
            sp.wait_ge(cleared, 2)
            sp.dma_start(w2[0:D, 0:D], w).then_inc(w_in, 16)
            sp.dma_start(w2[D:P, D:P], w).then_inc(w_in, 16)
            for pair in range(PAIRS):
                sp.dma_start(xtp[:, pair, 2:], xt[pair, :, 1:]).then_inc(xt_in, 16)
            for k in range(NB):
                for half in range(2):
                    if k >= 1:
                        sp.wait_ge(adj_used, 2 * k + half - 1)
                    sp.dma_start(adjb[:, half, :], adj[k * P:(k + 1) * P, half * HALF:(half + 1) * HALF])\
                      .then_inc(adj_in[half], 16)

        @block.gpsimd
        def _(pool):
            nc.gpsimd.memset(w2[:], 0.0).then_inc(cleared, 1)
            nc.gpsimd.memset(xtp[:, :, 0:2], 0.0).then_inc(cleared, 1)
            nc.gpsimd.memset(ones[:], 1.0).then_inc(id_ready, 1)
            nc.gpsimd.memset(half_power[:], -0.5).then_inc(id_ready, 1)
            nc.gpsimd.memset(ident[:], 0.0).then_inc(id_ready, 1)
            pool.wait_ge(id_ready, 3)
            nc.gpsimd.affine_select(out=ident[:], in_=ident[:], compare_op=ALU.not_equal, fill=1.0,
                                    base=0, pattern=[[-1, P]], channel_multiplier=1).then_inc(id_ready, 1)
            for k in range(NB):
                pool.wait_ge(var_ready, k + 1)
                nc.gpsimd.tensor_tensor(st[:, 2, :], st[:, 1, :], half_power[:, 0:B],
                                        ALU.pow).then_inc(pow_done, 1)

        @block.tensor
        def _(pe):
            pe.wait_ge(w_in, 32)
            pe.wait_ge(xt_in, 16 * PAIRS)
            pe.wait_ge(id_ready, 4)
            for k in range(NB):
                if k >= 1:
                    pe.wait_ge(hn_copied, k)
                for pair in range(PAIRS):
                    last = nc.tensor.matmul(ph[:, pair * P:(pair + 1) * P],
                                            xtp[:, pair, 1 + k * P:1 + (k + 1) * P], w2[:],
                                            start=True, stop=True)
                last.then_inc(h_ready, 1)
                if k >= 1:
                    pe.wait_ge(rest_ready, k)
                for pair in range(PAIRS):
                    last = nc.tensor.matmul(pshift[:, pair * P:(pair + 1) * P],
                                            xtp[:, pair, k * P:(k + 1) * P], w2[:],
                                            start=True, stop=True)
                last.then_inc(hs_ready, 1)
                pe.wait_ge(hn_copied, k + 1)
                last = nc.tensor.matmul(psum[:], ones[:], hn[:, k, :], start=(k == 0), stop=(k == NB - 1))
            last.then_inc(sum_ready, 1)
            for j in range(NB):
                pe.wait_ge(adj_used, 2 * j + 2)
                pe.wait_ge(parts_ready, j + 1)
                for i in range(JOUTER):
                    for part in range(3):
                        last = nc.tensor.matmul(acc[i][:], mask[:, j, i * P:(i + 1) * P],
                                                parts[:, part, j, :], start=(j == 0 and part == 0),
                                                stop=(j == NB - 1 and part == 2))
                    if j == NB - 1:
                        last.then_inc(acc_ready, 1)
            for i in range(JOUTER, NB):
                if i >= ACCS:
                    pe.wait_ge(acc_read, i - ACCS + 1)
                for j in range(NB):
                    for part in range(3):
                        last = nc.tensor.matmul(acc[i % ACCS][:], mask[:, j, i * P:(i + 1) * P],
                                                parts[:, part, j, :], start=(j == 0 and part == 0),
                                                stop=(j == NB - 1 and part == 2))
                last.then_inc(acc_ready, 1)

        @block.scalar
        def _(act):
            for k in range(2):
                act.dma_start(xb[:, k, :].rearrange("p (b d) -> p b d", b=B), xn[:, k]).then_inc(blk_in[k], 16)
                act.dma_start(ab[:, k, :], at[k * P:(k + 1) * P, :]).then_inc(blk_in[k], 16)
            for k in range(NB):
                act.wait_ge(h_ready, k + 1)
                nc.scalar.copy(hn[:, k, :], ph[:]).then_inc(hn_copied, 1)
                act.wait_ge(hs_ready, k + 1)
                nc.scalar.copy(parts[:, 0, k, :], pshift[:]).then_inc(part1, 1)
            act.wait_ge(sum_ready, 1)
            nc.scalar.copy(hsum[:], psum[:]).then_inc(sum_copied, 1)
            for k in range(NB):
                act.wait_ge(x1_ready, k + 1)
                act.dma_start(x1n[:, k, 0:B], t1[:, k % 2, :].rearrange("p (b d) -> p b d", b=B))\
                   .then_inc(stored[k % 2], 16)
                act.dma_start(x1n[:, k, B], t1[:, k % 2, 0:D]).then_inc(stored[k % 2], 16)
                if k + 2 < NB:
                    act.wait_ge(blk_used, k + 1)
                    act.dma_start(xb[:, k % 2, :].rearrange("p (b d) -> p b d", b=B), xn[:, k + 2])\
                       .then_inc(blk_in[k % 2], 16)
                    act.dma_start(ab[:, k % 2, :], at[(k + 2) * P:(k + 3) * P, :]).then_inc(blk_in[k % 2], 16)
            for s in stored:
                act.wait_ge(s, 32 * NB // 2)

        @block.vector
        def _(dve):
            for k in range(NB):
                for half in range(2):
                    dve.wait_ge(adj_in[half], 16 * (k + 1))
                    nc.vector.tensor_scalar(mask[:, k, half * HALF:(half + 1) * HALF], adjb[:, half, :], 0,
                                            None, ALU.is_gt).then_inc(adj_used, 1)
                dve.wait_ge(part1, k + 1)
                r = rest[:, k % 2, :]
                nc.vector.tensor_tensor(r, pshift[:], parts[:, 0, k, :], ALU.subtract).then_inc(rest_ready, 1)
                drain_link(dve)
                nc.vector.tensor_copy(parts[:, 1, k, :], r)
                drain_link(dve)
                nc.vector.tensor_tensor(parts[:, 2, k, :], r, parts[:, 1, k, :], ALU.subtract)\
                  .then_inc(parts_ready, 1)
            dve.wait_ge(sum_copied, 1)
            for i in range(NB):
                t = t1[:, i % 2, :]
                t3 = t.rearrange("p (b d) -> p b d", b=B)
                dve.wait_ge(blk_in[i % 2], 32 * (i // 2 + 1))
                if i >= 2:
                    dve.wait_ge(stored[i % 2], 32 * (i // 2))
                a1 = ab[:, i % 2, 0:D].unsqueeze(1).to_broadcast([P, B, D])
                a2 = ab[:, i % 2, D:2 * D].unsqueeze(1).to_broadcast([P, B, D])
                drain_link(dve)
                nc.vector.tensor_tensor(t3, hn[:, i, :].rearrange("p (b d) -> p b d", b=B), a1, ALU.mult)
                dve.wait_ge(acc_ready, i + 1)
                nc.vector.tensor_tensor(t2[:].rearrange("p (b d) -> p b d", b=B),
                                        acc[i % ACCS][:].rearrange("p (b d) -> p b d", b=B), a2,
                                        ALU.mult).then_inc(acc_read, 1)
                drain_link(dve)
                nc.vector.tensor_tensor(t, t, t2[:], ALU.add)
                drain_link(dve)
                nc.vector.tensor_reduce(score[:], t3, axis=X_AXIS, op=ALU.add)
                drain_link(dve)
                if i == 0:
                    nc.vector.memset(score[0:1, :], 0.0)
                    drain_link(dve)
                nc.vector.tensor_tensor(t3, hsum[:].rearrange("p (b d) -> p b d", b=B),
                                        score[:].unsqueeze(2).to_broadcast([P, B, D]), ALU.mult)
                drain_link(dve)
                nc.vector.scalar_tensor_tensor(out=t, in0=t, scalar=0.2, in1=t, op0=ALU.mult, op1=ALU.max)
                drain_link(dve)
                nc.vector.tensor_tensor(t, t, xb[:, i % 2, :], ALU.add).then_inc(blk_used, 1)
                norm_start(nc, dve, t3, t2[:].rearrange("p (b d) -> p b d", b=B), st[:, 0, :], st[:, 1, :],
                           B, var_ready)
                dve.wait_ge(pow_done, i + 1)
                nc.vector.tensor_tensor(t3, t3, spread(st[:, 2, :], B), ALU.mult).then_inc(x1_ready, 1)
            for k in range(NB):
                nc.vector.tensor_scalar(mask[:, k, :], mask[:, k, :], -1.0, -MASKED, ALU.add, ALU.mult)
            drain_link(dve)
            dblocks = diagonal_blocks(mask)
            nc.vector.tensor_tensor(diag[:], dblocks, ident[:].unsqueeze(1).to_broadcast([P, NB, P]), ALU.mult)
            drain_link(dve)
            nc.vector.tensor_tensor(dblocks, dblocks, diag[:], ALU.subtract)


def diagonal_blocks(mask):
    return bass.AP(mask[:].tensor, 0, [[NB * N, P], [N + P, NB], [1, P]])


def attention_layers(nc, x1, out, whd, bh, wod, bo, gamma, beta, w2, a2, w3, a3,
                     mask, ident, half_power, diag):
    ctx = ExitStack()
    with ctx:
        def sb(name, shape, dt):
            return ctx.enter_context(nc.sbuf_tensor(name, shape, dt))

        def sem(name):
            return ctx.enter_context(nc.semaphore(name))

        xin = sb("xin", [P, NB, D], F32)
        xb = sb("xb", [P, NB, D], F32)
        xz = sb("xz", [P, N], F32)
        xt = xz[0:D, :]
        zt = xz[:].rearrange("p (i k n) -> p i k n", i=2, k=2)
        xc = sb("xc", [D, BANK], F32)
        y = sb("y", [P, NB, D], F32)
        tmp = sb("tmp", [P, CH, D], F32)
        z = sb("z", [P, NB, H * D], F32)
        ha = [sb(f"ha{i}", [P, N], F32R) for i in range(2)]
        hb = [sb(f"hb{i}", [P, N], F32R) for i in range(2)]
        hn = [sb(f"hn{i}", [P, NB, D], F32) for i in range(3)]
        rows = sb("rows", [P, RING, N], F32)
        sr = sb("sr", [P, N], F32)
        pt = sb("pt", [P, 2, N], F32)
        nm = sb("nm", [P, NB, 2], F32)
        rs = sb("rs", [P, NB], F32)
        rc = sb("rc", [P, NB], F32)
        whf = sb("whf", [P, H * 2 * D], F32)
        wh = whf[0:D, :].rearrange("p (h n) -> p h n", h=H)
        hf = whf[D:P, :]
        wo = sb("wo", [P, 2, 2 * D], F32)
        wl = sb("wl", [D, 2, D + 2], F32)
        bhs = sb("bhs", [P, H, D], F32)
        bos = sb("bos", [P, D], F32)
        gam = sb("gam", [P, D], F32)
        bet = sb("bet", [P, D], F32)
        st = sb("st", [P, 3, NB], F32)
        ls = sb("ls", [P, 2, NB], F32)
        rt = sb("rt", [P, NB], F32)
        av = y[0:D, 0:4, :]
        wa = y[0:D, 4:5, :]

        pss = ctx.enter_context(nc.psum_tensor("pss", [P, N], F32))
        tp = [ctx.enter_context(nc.psum_tensor(f"tp{i}", [P, BANK], F32)) for i in range(2)]
        po = ctx.enter_context(nc.psum_tensor("po", [P, BANK], F32))
        px = ctx.enter_context(nc.psum_tensor("px", [P, BANK], F32))

        gates = sem("gates")
        const_in = sem("const_in")
        slopes_set = sem("slopes_set")
        xin_in = sem("xin_in")
        xb_in = sem("xb_in")
        x_done = sem("x_done")
        x_out = sem("x_out")
        x_ready = sem("x_ready")
        xn_psum = sem("xn_psum")
        xn_ready = sem("xn_ready")
        xt_psum = sem("xt_psum")
        xt_ready = sem("xt_ready")
        z_ready = sem("z_ready")
        zt_psum = sem("zt_psum")
        zt_ready = sem("zt_ready")
        proj_psum = sem("proj_psum")
        h1_ready = sem("h1_ready")
        h2_ready = sem("h2_ready")
        hn_psum = sem("hn_psum")
        hn_ready = sem("hn_ready")
        lr_ready = sem("lr_ready")
        right_psum = sem("right_psum")
        sr_ready = sem("sr_ready")
        diag_set = sem("diag_set")
        scores_ready = sem("scores_ready")
        lift_ready = sem("lift_ready")
        mr_ready = sem("mr_ready")
        scores_read = sem("scores_read")
        exp_ready = sem("exp_ready")
        tr_ready = sem("tr_ready")
        pt_act = sem("pt_act")
        pt_dve = sem("pt_dve")
        pv_ready = sem("pv_ready")
        out_read = sem("out_read")
        var_ready = sem("var_ready")
        pow_done = sem("pow_done")
        block = ctx.enter_context(nc.Block())

        CONSTS = 10
        ROWS = LOOP.blocks
        TASKS = LOOP.tally

        @block.sync
        def _(sp):
            for tile, src in (
                (wh, whd.rearrange("h c n -> c h n")),
                (wo[:], wod.rearrange("(k p) n -> p k n", p=P)),
                (wl[:, 0, 0:D], w2),
                (wl[:, 1, 0:D], w3),
                (av[:, 0:2, :], a2.rearrange("(o s d) -> o s d", o=1, s=2).to_broadcast([D, 2, D])),
                (av[:, 2:4, :], a3.rearrange("(o s d) -> o s d", o=1, s=2).to_broadcast([D, 2, D])),
                (bhs[:], bh.rearrange("(o h) d -> o h d", o=1).to_broadcast([P, H, D])),
                (bos[:], bo.rearrange("(o d) -> o d", o=1).to_broadcast([P, D])),
                (gam[:], gamma.rearrange("(o d) -> o d", o=1).to_broadcast([P, D])),
                (bet[:], beta.rearrange("(o d) -> o d", o=1).to_broadcast([P, D])),
            ):
                sp.dma_start(tile, src).then_inc(const_in, 16)
            sp.dma_start(xin[:], x1[0].rearrange("(k p) d -> p k d", p=P)).then_inc(xin_in, 16)
            sp.dma_start(xb[:], x1[0].rearrange("(k p) d -> p k d", p=P)).then_inc(xb_in, 16)
            sp.wait_ge(xn_psum, NC)
            sp.dma_start(xin[:], x1[1].rearrange("(k p) d -> p k d", p=P)).then_inc(xin_in, 16)
            with sp.Fori(0, B - 1) as b:
                stand_alone_wait(sp, xn_psum, b * NC + 2 * NC, gates)
                sp.dma_start(xin[:], x1[bass.ds(b + 2, 1)].rearrange("o (k p) d -> p (o k) d", p=P))\
                  .then_inc(xin_in, 16)
                dst = out[bass.ds(b, 1)].rearrange("o (k p) d -> p (o k) d", p=P)
                for c in range(NC):
                    blocks = slice(c * CH, (c + 1) * CH)
                    stand_alone_wait(sp, x_done, b * NC + c + 1, gates)
                    sp.dma_start(dst[:, blocks, :], xb[:, blocks, :]).then_inc(x_out, 16)
                stand_alone_wait(sp, x_out, b * (16 * NC) + 16 * NC, gates)
                sp.dma_start(xb[:], x1[bass.ds(b + 1, 1)].rearrange("o (k p) d -> p (o k) d", p=P))\
                  .then_inc(xb_in, 16)
            dst = out[B - 1].rearrange("(k p) d -> p k d", p=P)
            for c in range(NC):
                blocks = slice(c * CH, (c + 1) * CH)
                sp.wait_ge(x_done, (B - 1) * NC + c + 1)
                sp.dma_start(dst[:, blocks, :], xb[:, blocks, :]).then_inc(x_out, 16)
            sp.wait_ge(x_out, B * 16 * NC)
            sp.wait_ge(xin_in, 16 * (B + 1))

        @block.gpsimd
        def _(pool):
            norms = Count(var_ready, TASKS("lna", "lnb", "ra"))
            sr_c = Count(sr_ready, TASKS("r"))
            tr_c = Count(tr_ready, ROWS * NC)
            read_c = Count(scores_read, ROWS * 2)
            mr_c = Count(mr_ready, LOOP.adds)
            diag_c = Count(diag_set, TASKS("open", "close"))
            counts = (norms, sr_c, tr_c, read_c, mr_c, diag_c)

            def wait(count, n=None):
                stand_alone_wait(pool, count.sem, count.value(n), gates)

            def run_task(segment, name, unit, c):
                blocks = slice(c * CH, (c + 1) * CH)
                if name in ("lna", "lnb", "ra"):
                    norms.n += 1
                    wait(norms)
                    nc.gpsimd.tensor_tensor(st[:, 2, blocks], st[:, 1, blocks], half_power[:, 0:CH], ALU.pow)\
                      .then_inc(pow_done, 1)
                elif name == "r":
                    sr_c.n += 1
                elif name in ("close", "open"):
                    last = [r for r in segment.rows if r and r.k == unit][0]
                    if last.gat:
                        wait(read_c, read_c.n + 2 * last.k + 2)
                    else:
                        wait(mr_c, mr_c.n + last.nth + 1)
                    view = diagonal_blocks(mask)[:, blocks, :]
                    nc.gpsimd.tensor_tensor(view, view, diag[:, blocks, :],
                                            ALU.add if name == "close" else ALU.subtract).then_inc(diag_set, 1)
                    diag_c.n += 1

            def mask_row(row):
                if row.t == 0:
                    wait(sr_c)
                if row.unit == ADD2 and row.t % CH == 0:
                    wait(diag_c)
                wait(tr_c, tr_c.n + NC * (row.slot_user + 1))
                nc.gpsimd.tensor_tensor(rows[:, row.slot, :], sr[:], mask[:, row.t, :], ALU.add)\
                  .then_inc(mr_ready, 1)

            def run_segment(segment):
                for task in segment.tasks.get("before", ()):
                    run_task(segment, *task)
                for s in segment.steps:
                    row = segment.row(s + 1)
                    if row and not row.gat and row.t > 0:
                        mask_row(row)
                    for task in segment.tasks.get(s, ()):
                        run_task(segment, *task)
                    if row and not row.gat and row.t == 0:
                        mask_row(row)
                for task in segment.tasks.get("after", ()):
                    run_task(segment, *task)
                tr_c.n += NC * segment.blocks
                read_c.n += 2 * segment.blocks
                mr_c.n += segment.adds

            pool.sem_inc(diag_set, TASKS("open", "close"))
            diag_c.n += TASKS("open", "close")
            run_segments(pool, counts, run_segment)

        @block.tensor
        def _(pe):
            xin_c = Count(xin_in, 16)
            xr_c = Count(x_ready, TASKS("xt"))
            xn_c = Count(xn_ready, TASKS("xn"))
            xt_c = Count(xt_ready, TASKS("xt"))
            z_c = Count(z_ready, H * NC)
            zt_c = Count(zt_ready, TASKS("z0", "z1"))
            h2_c = Count(h2_ready, TASKS("proj"))
            hn_c = Count(hn_ready, TASKS("hn", "h"))
            lr_c = Count(lr_ready, TASKS("h"))
            sr_c = Count(sr_ready, TASKS("r"))
            read_c = Count(scores_read, ROWS * 2)
            exp_c = Count(exp_ready, ROWS)
            copied = {"act": Count(pt_act, LOOP.act_tiles), "dve": Count(pt_dve, LOOP.dve_tiles)}
            out_c = Count(out_read, ROWS)
            counts = (xin_c, xr_c, xn_c, xt_c, z_c, zt_c, h2_c, hn_c, lr_c, sr_c, read_c, exp_c, copied["act"],
                      copied["dve"], out_c)
            px_reader = [None]

            def wait(count, n=None):
                stand_alone_wait(pe, count.sem, count.value(n), gates)

            def wait_copy(row, q):
                count = copied[row.copier[q]]
                wait(count, count.n + row.count[q] + 1)

            def px_free():
                if px_reader[0] is not None:
                    wait(px_reader[0])

            def px_used(count):
                count.n += 1
                px_reader[0] = count

            def run_task(name, unit, c):
                cols = slice(c * BANK, (c + 1) * BANK)
                if name == "xn":
                    px_free()
                    if c == 0:
                        xin_c.n += 16
                        wait(xin_c)
                    for q in range(CH):
                        last = nc.tensor.transpose(px[0:D, q * P:(q + 1) * P], xin[:, c * CH + q, :], ident[:])
                    last.then_inc(xn_psum, 1)
                    px_used(xn_c)
                elif name == "xt":
                    px_free()
                    xr_c.n += 1
                    wait(xr_c)
                    for q in range(CH):
                        last = nc.tensor.transpose(px[0:D, q * P:(q + 1) * P], xb[:, c * CH + q, :], ident[:])
                    last.then_inc(xt_psum, 1)
                    px_used(xt_c)
                elif name in ("z0", "z1"):
                    k = int(name[1])
                    px_free()
                    if k == 0:
                        z_c.n += 1 if c else (H - 1) * NC + 1
                        wait(z_c)
                    for q in range(CH):
                        last = nc.tensor.transpose(px[:, q * P:(q + 1) * P],
                                                   z[:, c * CH + q, k * P:(k + 1) * P], ident[:])
                    last.then_inc(zt_psum, 1)
                    px_used(zt_c)
                elif name == "proj":
                    px_free()
                    if unit == GAT2:
                        wait(zt_c)
                        for k in range(2):
                            last = nc.tensor.matmul(px[:], wo[:, k, :], zt[:, c % 2, k, :],
                                                    start=(k == 0), stop=(k == 1))
                    else:
                        wait(xn_c)
                        last = nc.tensor.matmul(px[:], wh[:, unit, :], xt[:, cols], start=True, stop=True)
                    last.then_inc(proj_psum, 1)
                    px_used(h2_c)
                elif name == "hn":
                    px_free()
                    for q in range(CH):
                        last = nc.tensor.transpose(px[:, q * D:(q + 1) * D], hf[:, q * P:(q + 1) * P],
                                                   ident[D:P, D:P])
                    last.then_inc(hn_psum, 1)
                    px_used(hn_c)
                elif name == "h":
                    px_free()
                    wait(xt_c)
                    for q in range(CH):
                        last = nc.tensor.matmul(px[:, q * (D + 2):(q + 1) * (D + 2)], xc[:, q * P:(q + 1) * P],
                                                wl[:, unit - ADD1, :], start=True, stop=True)
                    last.then_inc(hn_psum, 1)
                    px_used(lr_c)
                    hn_c.n += 1
                elif name == "r":
                    px_free()
                    wait(lr_c)
                    for q in range(CH):
                        k = c * CH + q
                        last = nc.tensor.transpose(px[:, q * P:(q + 1) * P],
                                                   rt[:, k:k + 1].to_broadcast([P, P]), ident[:])
                    last.then_inc(right_psum, 1)
                    px_used(sr_c)

            def dot_products(row):
                i, rows_t = PROJ[row.unit], slice(row.t * P, (row.t + 1) * P)
                if row.t == 0:
                    wait(h2_c)
                for half in range(2):
                    if row.k:
                        wait(read_c, read_c.n + 2 * (row.k - 1) + half + 1)
                    for c in range(half * NC // 2, (half + 1) * NC // 2):
                        cols = slice(c * BANK, (c + 1) * BANK)
                        moving = ha[i][:, cols]
                        nc.tensor.matmul(pss[:, cols], ha[i][:, rows_t], moving, start=True, stop=False)
                        last = nc.tensor.matmul(pss[:, cols], hb[i][:, rows_t], moving, start=False, stop=True)
                    last.then_inc(scores_ready, 1)

            def run_segment(segment):
                for task in segment.tasks.get("before", ()):
                    run_task(*task)
                for s in segment.steps:
                    row, turned, summed = (segment.row(s - n) for n in range(3))
                    if row and row.gat:
                        dot_products(row)
                    if row and row.t == 0:
                        wait(hn_c)
                    for task in segment.tasks.get(s, ()):
                        run_task(*task)
                    for q in range(NC):
                        if summed:
                            wait_copy(summed, q)
                            if q == 0 and (summed.k or out_c.n):
                                wait(out_c, out_c.n + summed.k)
                            for jb in range(CH * q, CH * (q + 1)):
                                last = nc.tensor.matmul(po[:, 0:D], pt[:, summed.k % 2, jb * P:(jb + 1) * P],
                                                        hn[summed.hn][:, jb, :], start=(jb == 0),
                                                        stop=(jb == NB - 1))
                            if q == NC - 1:
                                last.then_inc(pv_ready, 1)
                        if turned:
                            if q == 0:
                                wait(exp_c, exp_c.n + turned.k + 1)
                            if q >= 2:
                                wait_copy(turned, q - 2)
                            elif turned.k:
                                wait_copy(turned.before, q + 2)
                            for r in range(CH):
                                jb = CH * q + r
                                last = nc.tensor.transpose(tp[q % 2][:, r * P:(r + 1) * P],
                                                           rows[:, turned.slot, jb * P:(jb + 1) * P], ident[:])
                            last.then_inc(tr_ready, 1)
                for task in segment.tasks.get("after", ()):
                    run_task(*task)
                exp_c.n += segment.blocks
                out_c.n += segment.blocks
                read_c.n += 2 * segment.blocks
                copied["act"].n += segment.act_tiles
                copied["dve"].n += segment.dve_tiles

            pe.wait_ge(const_in, 16 * CONSTS)
            pe.wait_ge(slopes_set, 1)
            run_segments(pe, counts, run_segment)

        @block.scalar
        def _(act):
            xn_c = Count(xn_psum, TASKS("xn"))
            xt_c = Count(xt_psum, TASKS("xt"))
            zt_c = Count(zt_psum, TASKS("z0", "z1"))
            proj_c = Count(proj_psum, TASKS("proj"))
            hn_c = Count(hn_psum, TASKS("hn", "h"))
            right_c = Count(right_psum, TASKS("r"))
            sr_c = Count(sr_ready, TASKS("r"))
            lr_c = Count(lr_ready, TASKS("h"))
            read_c = Count(scores_read, ROWS * 2)
            tr_c = Count(tr_ready, ROWS * NC)
            pv_c = Count(pv_ready, ROWS)
            counts = (xn_c, xt_c, zt_c, proj_c, hn_c, right_c, sr_c, lr_c, read_c, tr_c, pv_c)

            def wait(count, n=None):
                stand_alone_wait(act, count.sem, count.value(n), gates)

            def next_of(count):
                count.n += 1
                wait(count)

            def run_task(name, unit, c):
                cols = slice(c * BANK, (c + 1) * BANK)
                blocks = slice(c * CH, (c + 1) * CH)
                if name == "xn":
                    next_of(xn_c)
                    nc.scalar.copy(xt[:, cols], px[0:D, :]).then_inc(xn_ready, 1)
                elif name == "xt":
                    next_of(xt_c)
                    nc.scalar.copy(xc[:], px[0:D, :]).then_inc(xt_ready, 1)
                elif name in ("z0", "z1"):
                    next_of(zt_c)
                    nc.scalar.copy(zt[:, c % 2, int(name[1]), :], px[:]).then_inc(zt_ready, 1)
                elif name == "proj":
                    i = PROJ[unit]
                    next_of(proj_c)
                    nc.scalar.copy(ha[i][0:D, cols], px[0:D, :])
                    nc.scalar.copy(hb[i][D:P, cols], px[D:P, :])
                    nc.scalar.copy(hf, px[D:P, :]).then_inc(h1_ready, 1)
                elif name == "hn":
                    next_of(hn_c)
                    nc.scalar.copy(hn[hn_of(unit)][:, blocks, :],
                                   px[:, 0:CH * D].rearrange("p (k d) -> p k d", d=D)).then_inc(hn_ready, 1)
                elif name == "h":
                    next_of(hn_c)
                    lr_c.n += 1
                    nc.scalar.copy(hn[hn_of(unit)][:, blocks, :],
                                   px[:, 0:CH * (D + 2)].rearrange("p (k d) -> p k d", d=D + 2)[:, :, 0:D])\
                      .then_inc(hn_ready, 1)
                elif name == "r":
                    next_of(right_c)
                    sr_c.n += 1
                    nc.scalar.mul(sr[:, cols], px[:], SLOPES[unit]).then_inc(sr_ready, 1)

            where = [None]

            def hn_of(unit):
                return [r.hn for r in where[0].rows if r and r.unit == unit][0]

            def copy_tile(row, q):
                if not row or row.copier[q] != "act":
                    return
                if q == 0 and (row.k >= 2 or pv_c.n):
                    wait(pv_c, pv_c.n + row.k - 1)
                wait(tr_c, tr_c.n + NC * row.k + q + 1)
                nc.scalar.copy(pt[:, row.k % 2, q * BANK:(q + 1) * BANK], tp[q % 2][:]).then_inc(pt_act, 1)

            def lift_row(row):
                slope = SLOPES[row.unit]
                if row.t == 0:
                    wait(lr_c)
                    wait(sr_c)
                for half in range(2):
                    cols = slice(half * HALF, (half + 1) * HALF)
                    wait(read_c, read_c.n + 2 * (row.k - 1) + half + 1)
                    nc.scalar.activation(pss[:, cols], sr[:, cols], ACT.Relu, scale=(1.0 - slope) / slope,
                                         bias=ls[:, row.unit - ADD1, row.t:row.t + 1]).then_inc(lift_ready, 1)

            def run_segment(segment):
                where[0] = segment
                for task in segment.tasks.get("before", ()):
                    run_task(*task)
                for s in segment.steps:
                    row, turned, following = segment.row(s), segment.row(s - 1), segment.row(s + 1)
                    additive = row and not row.gat
                    for task in segment.tasks.get(s, ()):
                        run_task(*task)
                    copy_tile(turned, 0)
                    copy_tile(turned, 1)
                    if additive and following and not following.gat:
                        lift_row(following)
                    if row:
                        wait(read_c, read_c.n + 2 * row.k + 2)
                        nc.scalar.activation(rows[:, row.slot, :], rows[:, row.slot, :], ACT.Exp, scale=-1.0,
                                             bias=nm[:, row.t, 1:2], accum_out=rs[:, row.t:row.t + 1])\
                          .then_inc(exp_ready, 1)
                    copy_tile(turned, 2)
                    copy_tile(turned, 3)
                    if not additive and following and not following.gat:
                        lift_row(following)
                for task in segment.tasks.get("after", ()):
                    run_task(*task)
                read_c.n += 2 * segment.blocks
                tr_c.n += NC * segment.blocks
                pv_c.n += segment.blocks

            run_segments(act, counts, run_segment)

        @block.vector
        def _(dve):
            h1_c = Count(h1_ready, TASKS("proj"))
            hn_c = Count(hn_ready, TASKS("hn", "h"))
            xb_c = Count(xb_in, 16)
            pow_c = Count(pow_done, TASKS("lna", "lnb", "ra"))
            diag_c = Count(diag_set, TASKS("open", "close"))
            scores_c = Count(scores_ready, LOOP.gats * 2)
            lift_c = Count(lift_ready, LOOP.adds * 2)
            mr_c = Count(mr_ready, LOOP.adds)
            tr_c = Count(tr_ready, ROWS * NC)
            pv_c = Count(pv_ready, ROWS)
            counts = (h1_c, hn_c, xb_c, pow_c, diag_c, scores_c, lift_c, mr_c, tr_c, pv_c)

            def wait(count, n=None):
                stand_alone_wait(dve, count.sem, count.value(n), gates)

            def next_of(count):
                count.n += 1
                wait(count)

            def each(v):
                return v[:].unsqueeze(1).to_broadcast([P, CH, D])

            def run_task(name, unit, c):
                cols = slice(c * BANK, (c + 1) * BANK)
                blocks = slice(c * CH, (c + 1) * CH)
                yc, xbc, sq = y[:, blocks, :], xb[:, blocks, :], tmp[:]
                sums, var, rstd = (st[:, n, blocks] for n in range(3))
                if name == "proj":
                    i = PROJ[unit]
                    next_of(h1_c)
                    nc.vector.tensor_tensor(ha[i][D:P, cols], px[D:P, :], hb[i][D:P, cols].bitcast(F32),
                                            ALU.subtract)
                    nc.vector.tensor_tensor(hb[i][0:D, cols], px[0:D, :], ha[i][0:D, cols].bitcast(F32),
                                            ALU.subtract).then_inc(h2_ready, 1)
                elif name == "hn":
                    hn_c.n += 1
                elif name == "h":
                    next_of(hn_c)
                    pair = px[:, 0:CH * (D + 2)].rearrange("p (k d) -> p k d", d=D + 2)
                    nc.vector.tensor_scalar(ls[:, unit - ADD1, blocks].unsqueeze(2), pair[:, :, D:D + 1],
                                            1.0 - SLOPES[unit], None, ALU.mult)
                    nc.vector.tensor_copy(rt[:, blocks].unsqueeze(2), pair[:, :, D + 1:D + 2])\
                      .then_inc(lr_ready, 1)
                elif name == "lna":
                    drain_link(dve)
                    nc.vector.scalar_tensor_tensor(out=yc, in0=yc, scalar=0.2, in1=yc, op0=ALU.mult,
                                                   op1=ALU.max)
                    norm_start(nc, dve, yc, sq, sums, var, CH, var_ready)
                elif name == "lnb":
                    next_of(pow_c)
                    nc.vector.tensor_tensor(yc, yc, spread(rstd, CH), ALU.mult)
                    drain_link(dve)
                    nc.vector.tensor_tensor(yc, yc, each(gam), ALU.mult)
                    drain_link(dve)
                    nc.vector.tensor_tensor(yc, yc, each(bet), ALU.add)
                    if c == 0:
                        xb_c.n += 16
                        wait(xb_c)
                    drain_link(dve)
                    nc.vector.tensor_tensor(xbc, xbc, yc, ALU.add)
                    norm_start(nc, dve, xbc, sq, sums, var, CH, var_ready)
                elif name in ("lnc", "rb"):
                    next_of(pow_c)
                    drain_link(dve)
                    nc.vector.tensor_tensor(xbc, xbc, spread(rstd, CH), ALU.mult)\
                      .then_inc(x_done if unit == ADD2 else x_ready, 1)
                elif name == "ra":
                    drain_link(dve)
                    nc.vector.tensor_tensor(xbc, xbc, yc, ALU.add)
                    norm_start(nc, dve, xbc, sq, sums, var, CH, var_ready)

            def masked_scores(row):
                if row.gat:
                    if row.slot_user >= 0 or tr_c.n:
                        wait(tr_c, tr_c.n + NC * (row.slot_user + 1))
                else:
                    wait(mr_c, mr_c.n + row.nth + 1)
                for half in range(2):
                    cols = slice(half * HALF, (half + 1) * HALF)
                    scores = rows[:, row.slot, cols]
                    count = scores_c if row.gat else lift_c
                    wait(count, count.n + 2 * row.nth + half + 1)
                    nc.vector.tensor_tensor_reduce(
                        out=scores, in0=pss[:, cols], in1=mask[:, row.t, cols] if row.gat else scores,
                        scale=-1.0, scalar=(-2 * MASKED if half == 0 else nm[:, row.t, 0:1]),
                        op0=ALU.add, op1=ALU.min, accum_out=nm[:, row.t, half:half + 1]).then_inc(scores_read, 1)
                    if half == 0:
                        drain_link(dve)

            def copy_tile(row, q):
                if not row or row.copier[q] != "dve":
                    return
                if q == 1:
                    wait(pv_c, pv_c.n + row.k - 1)
                wait(tr_c, tr_c.n + NC * row.k + q + 1)
                nc.vector.tensor_copy(pt[:, row.k % 2, q * BANK:(q + 1) * BANK], tp[q % 2][:]).then_inc(pt_dve, 1)

            def divide(row):
                t, unit = row.t, row.unit
                wait(pv_c, pv_c.n + row.k + 1)
                nc.vector.reciprocal(rc[:, t:t + 1], rs[:, t:t + 1])
                drain_link(dve)
                if row.gat:
                    dst, bias = (z[:, t, unit * D:(unit + 1) * D], bhs[:, unit, :]) if unit < H else \
                                (y[:, t, :], bos[:])
                    nc.vector.scalar_tensor_tensor(out=dst, in0=po[:, 0:D], scalar=rc[:, t:t + 1], in1=bias,
                                                   op0=ALU.mult, op1=ALU.add).then_inc(out_read, 1)
                else:
                    nc.vector.tensor_scalar(y[:, t, :], po[:, 0:D], rc[:, t:t + 1], None, ALU.mult)\
                      .then_inc(out_read, 1)
                if unit < H and t % CH == CH - 1:
                    part = z[:, t + 1 - CH:t + 1, unit * D:(unit + 1) * D]
                    drain_link(dve)
                    nc.vector.scalar_tensor_tensor(out=part, in0=part, scalar=0.2, in1=part, op0=ALU.mult,
                                                   op1=ALU.max).then_inc(z_ready, 1)

            def run_segment(segment):
                for task in segment.tasks.get("before", ()):
                    run_task(*task)
                for s in segment.steps:
                    row, turned, summed = (segment.row(s - n) for n in range(3))
                    if row:
                        if row.unit == GAT2 and row.t == 0 and segment is LOOP:
                            wait(diag_c, diag_c.n + TASKS("close") + 1)
                        if row.unit == GAT2 and row.t == CH:
                            wait(diag_c, diag_c.n)
                        masked_scores(row)
                    copy_tile(turned, 1)
                    for task in segment.tasks.get(s, ()):
                        run_task(*task)
                    if summed:
                        divide(summed)
                    copy_tile(turned, 3)
                for task in segment.tasks.get("after", ()):
                    run_task(*task)
                tr_c.n += NC * segment.blocks
                pv_c.n += segment.blocks
                scores_c.n += 2 * segment.gats
                lift_c.n += 2 * segment.adds
                mr_c.n += segment.adds
                diag_c.n += segment.tally("open", "close")
                drain_link(dve)

            dve.wait_ge(const_in, 16 * CONSTS)
            for k in range(2):
                for side in range(2):
                    drain_link(dve)
                    nc.vector.tensor_tensor(wa, wl[:, k:k + 1, 0:D], av[:, 2 * k + side:2 * k + side + 1, :],
                                            ALU.mult)
                    drain_link(dve)
                    last = nc.vector.tensor_reduce(wl[:, k, D + side:D + side + 1], wa, axis=X_AXIS, op=ALU.add)
            last.then_inc(slopes_set, 1)
            diag_c.n += TASKS("open", "close")
            run_segments(dve, counts, run_segment)


def build(nc, x, xt, adj, w0, a0, whd, bh, wod, bo, gamma, beta, w2, a2, w3, a3, out):
    x1 = nc.dram_tensor("x1", [B + 1, N, D], F32).ap()
    with ExitStack() as ctx:
        mask = ctx.enter_context(nc.sbuf_tensor("mask", [P, NB, N], BF16))
        diag = ctx.enter_context(nc.sbuf_tensor("diag", [P, NB, P], BF16))
        ident = ctx.enter_context(nc.sbuf_tensor("ident", [P, P], F32))
        half_power = ctx.enter_context(nc.sbuf_tensor("half_power", [P, NB], F32))
        gated_sum_layer(nc, x, xt, adj, w0, a0, x1, mask, ident, half_power, diag, None)
        attention_layers(nc, x1, out, whd, bh, wod, bo, gamma, beta, w2, a2, w3, a3,
                         mask, ident, half_power, diag)


def kernel(x, adj, L0_gnn_W, L0_gnn_a, L1_gnn_Wh, L1_gnn_bh, L1_gnn_Wo, L1_gnn_bo, L1_gnn_gamma,
           L1_gnn_beta, L2_gnn_weight, L2_gnn_a, L3_gnn_W, L3_gnn_a):
    import numpy as np
    import concourse.bacc as bacc
    from concourse.bass_utils import run_bass_kernel_spmd as run

    def c(v):
        return np.ascontiguousarray(v)

    x = np.asarray(x)
    wh = np.asarray(L1_gnn_Wh).transpose(0, 2, 1)
    wo = np.asarray(L1_gnn_Wo).T
    arrays = {
        "x": c(x),
        "xt": c(x.transpose(0, 2, 1).reshape(B // 2, 2 * D, N)),
        "adj": c(adj),
        "w0": c(L0_gnn_W),
        "a0": c(np.asarray(L0_gnn_a).T),
        "whd": c(np.concatenate([wh, wh], axis=2)),
        "bh": c(L1_gnn_bh),
        "wod": c(np.concatenate([wo, wo], axis=1)),
        "bo": c(L1_gnn_bo),
        "gamma": c(L1_gnn_gamma),
        "beta": c(L1_gnn_beta),
        "w2": c(L2_gnn_weight),
        "a2": c(np.asarray(L2_gnn_a).reshape(-1)),
        "w3": c(L3_gnn_W),
        "a3": c(L3_gnn_a),
    }
    nc = bacc.Bacc("TRN2", target_bir_lowering=False, num_devices=1)
    args = [nc.dram_tensor(f"in_{n}", a.shape, mybir.dt.from_np(a.dtype), kind="ExternalInput").ap()
            for n, a in arrays.items()]
    out = nc.dram_tensor("out_0", [B, N, D], F32, kind="ExternalOutput").ap()
    build(nc, *args, out)
    r = run(nc, [{f"in_{n}": a for n, a in arrays.items()}], core_ids=[0])
    return r.results[0]["out_0"]
```
